# Optimizing a Trainium2 kernel written in Bass

```python
import numpy as np
import jax
import jax.numpy as jnp

def _softmax(x, axis=-1):
    return jax.nn.softmax(x, axis=axis)

def _gelu(x):
    return jax.nn.gelu(x, approximate=True)

def _silu(x):
    return jax.nn.silu(x)

def _sigmoid(x):
    return jax.nn.sigmoid(x)

def _layernorm(x, axis=-1, eps=1e-05):
    m = jnp.mean(x, axis=axis, keepdims=True)
    v = jnp.var(x, axis=axis, keepdims=True)
    return (x - m) / jnp.sqrt(v + eps)

def _scatter_add(tgt, idx, src, axis=0):
    return tgt.at[idx].add(src)

def _segment_sum(src, seg, n):
    return jax.ops.segment_sum(src, seg, n)
kernel_name = 'mk_xattn_ffn_d1_seqx_r8_facbec'

def setup_inputs(seed: int=0):
    np.random.seed(seed)
    _w = jnp.asarray

    def _rec_inputs():
        import jax
        import jax.numpy as jnp
        _rk = jax.random.key(seed)
        x = 0.0003765 + 1 * jax.random.normal(jax.random.fold_in(_rk, 1), (4, 256, 128), jnp.float32)
        _lenS = 256 - jax.random.randint(jax.random.fold_in(_rk, 7), (4,), 0, max(1, 256 // 4) + 1, jnp.int32)
        _lenS2 = 512 - jax.random.randint(jax.random.fold_in(_rk, 8), (4,), 0, max(1, 512 // 4) + 1, jnp.int32)
        _ctx_1024P = jax.random.normal(jax.random.fold_in(_rk, 11), (4, 16, 128), jnp.float32)
        _ctx_1024c = jax.random.dirichlet(jax.random.fold_in(_rk, 511), 0.3 * jnp.ones((16,), jnp.float32), (4, 512))
        _ctx_1024t = jnp.einsum('bsk,bkd->bsd', _ctx_1024c, _ctx_1024P)
        _ctx_1024t = _ctx_1024t * jax.lax.rsqrt(jnp.mean(jnp.square(_ctx_1024t)) + 1e-12) * 0.953939
        ctx_1024 = -0.000292821 + 1.00034 * (_ctx_1024t + 0.3 * jax.random.normal(jax.random.fold_in(_rk, 611), (4, 512, 128), jnp.float32))
        _validS = jnp.arange(256)[None, :] < _lenS[:, None]
        _validS2 = jnp.arange(512)[None, :] < _lenS2[:, None]
        _causal = jnp.tril(jnp.ones((256, 256), dtype=bool))
        mask_Bx1xSxS2_ik1 = jnp.where(jnp.broadcast_to(_validS2[:, None, None, :], (4, 1, 256, 512)), 1, 0).astype(jnp.int32)
        return (x, ctx_1024, mask_Bx1xSxS2_ik1)
    x, ctx_1024, mask_Bx1xSxS2_ik1 = _rec_inputs()

    def _L0_xattn_setup():
        import jax, jax.numpy as jnp
        import numpy as np
        HEADS = 16
        key = jax.random.key(seed)
        k1, k2, k3, k4, k5, k6 = jax.random.split(key, 6)
        N, L, E = (2, 256, 128)
        return {'values': jax.random.normal(k1, (N, L, E), dtype=jnp.float32), 'key': jax.random.normal(k2, (N, L, E), dtype=jnp.float32), 'query': jax.random.normal(k3, (N, L, E), dtype=jnp.float32), 'mask': jax.random.randint(k4, (N, 1, L, L), 0, 2, dtype=jnp.int32), 'W_out': jax.random.normal(k5, (E, E), dtype=jnp.float32) / np.sqrt(E), 'b_out': jax.random.normal(k6, (E,), dtype=jnp.float32) * 0.01}
    _L0_xattn_all = _L0_xattn_setup()
    _L0_xattn_in = {k: v for k, v in _L0_xattn_all.items() if k in ('W_out', 'b_out')}
    del _L0_xattn_all

    def _L0_ffn_setup():
        import jax, jax.numpy as jnp
        import numpy as np
        DIM = 128
        INTER = 256
        E = 8
        TOPK = 2
        ROUTE_SCALE = 1.0

        def _mlp(x, w1, w2, w3):
            h = jax.nn.silu(x @ w1.T) * (x @ w3.T)
            return h @ w2.T
        key = jax.random.key(seed)
        ks = jax.random.split(key, 10)
        s_in = 0.02
        return {'x': jax.random.normal(ks[0], (4, 256, DIM), dtype=jnp.float32), 'gate_w': jax.random.normal(ks[1], (E, DIM), dtype=jnp.float32) * s_in, 'gate_bias': jax.random.normal(ks[2], (E,), dtype=jnp.float32) * 0.01, 'w1': jax.random.normal(ks[3], (E, INTER, DIM), dtype=jnp.float32) * s_in, 'w2': jax.random.normal(ks[4], (E, DIM, INTER), dtype=jnp.float32) * s_in, 'w3': jax.random.normal(ks[5], (E, INTER, DIM), dtype=jnp.float32) * s_in, 'sw1': jax.random.normal(ks[6], (INTER, DIM), dtype=jnp.float32) * s_in, 'sw2': jax.random.normal(ks[7], (DIM, INTER), dtype=jnp.float32) * s_in, 'sw3': jax.random.normal(ks[8], (INTER, DIM), dtype=jnp.float32) * s_in}
    _L0_ffn_all = _L0_ffn_setup()
    _L0_ffn_in = {k: v for k, v in _L0_ffn_all.items() if k in ('gate_w', 'gate_bias', 'w1', 'w2', 'w3', 'sw1', 'sw2', 'sw3')}
    del _L0_ffn_all
    return {'x': x, 'ctx_1024': ctx_1024, 'mask_Bx1xSxS2_ik1': mask_Bx1xSxS2_ik1, 'L0_xattn_W_out': _L0_xattn_in['W_out'], 'L0_xattn_b_out': _L0_xattn_in['b_out'], 'L0_ffn_gate_w': _L0_ffn_in['gate_w'], 'L0_ffn_gate_bias': _L0_ffn_in['gate_bias'], 'L0_ffn_w1': _L0_ffn_in['w1'], 'L0_ffn_w2': _L0_ffn_in['w2'], 'L0_ffn_w3': _L0_ffn_in['w3'], 'L0_ffn_sw1': _L0_ffn_in['sw1'], 'L0_ffn_sw2': _L0_ffn_in['sw2'], 'L0_ffn_sw3': _L0_ffn_in['sw3']}

def reference(x, ctx_1024, mask_Bx1xSxS2_ik1, L0_xattn_W_out, L0_xattn_b_out, L0_ffn_gate_w, L0_ffn_gate_bias, L0_ffn_w1, L0_ffn_w2, L0_ffn_w3, L0_ffn_sw1, L0_ffn_sw2, L0_ffn_sw3):
    import jax
    import jax.numpy as jnp

    def _L0_xattn_ref(values, key, query, mask, W_out, b_out):
        import jax, jax.numpy as jnp
        import numpy as np
        HEADS = 16
        N, Lq, E = query.shape
        Lk = key.shape[1]
        H = HEADS
        D = E // H
        q = query.reshape(N, Lq, H, D)
        k = key.reshape(N, Lk, H, D)
        v = values.reshape(N, Lk, H, D)
        energy = jnp.einsum('nqhd,nkhd->nhqk', q, k)
        energy = jnp.where(mask == 0, jnp.float32(-1e+20), energy)
        attn = jax.nn.softmax(energy / np.float32(np.sqrt(D)), axis=3)
        out = jnp.einsum('nhqk,nkhd->nqhd', attn, v).reshape(N, Lq, H * D)
        return out @ W_out.T + b_out

    def _L0_ffn_ref(x, gate_w, gate_bias, w1, w2, w3, sw1, sw2, sw3):
        import jax, jax.numpy as jnp
        import numpy as np
        DIM = 128
        INTER = 256
        E = 8
        TOPK = 2
        ROUTE_SCALE = 1.0

        def _mlp(x, w1, w2, w3):
            h = jax.nn.silu(x @ w1.T) * (x @ w3.T)
            return h @ w2.T
        shape = x.shape
        xt = x.reshape(-1, DIM)
        T = xt.shape[0]
        logits = xt @ gate_w.T
        scores = jax.nn.softmax(logits.astype(jnp.float32), axis=-1)
        original_scores = scores
        biased = scores + gate_bias
        _, indices = jax.lax.top_k(biased, TOPK)
        weights = jnp.take_along_axis(original_scores, indices, axis=1)
        weights = (weights * ROUTE_SCALE).astype(x.dtype)
        combine = (jax.nn.one_hot(indices, E, dtype=weights.dtype) * weights[..., None]).sum(axis=1)
        y = jnp.zeros_like(xt)
        for e in range(E):
            y = y + _mlp(xt, w1[e], w2[e], w3[e]) * combine[:, e:e + 1]
        z = _mlp(xt, sw1, sw2, sw3)
        return (y + z).reshape(shape)
    x = x + _L0_xattn_ref(ctx_1024, ctx_1024, _layernorm(x, axis=-1), mask_Bx1xSxS2_ik1, L0_xattn_W_out, L0_xattn_b_out)
    x = x + _L0_ffn_ref(_layernorm(x, axis=-1), L0_ffn_gate_w, L0_ffn_gate_bias, L0_ffn_w1, L0_ffn_w2, L0_ffn_w3, L0_ffn_sw1, L0_ffn_sw2, L0_ffn_sw3)
    return x

_drawn_inputs = setup_inputs


def setup_inputs(seed=0):
    import zlib

    import numpy as np

    out = dict(_drawn_inputs(seed))
    spreads = {}
    factors = {'L0_xattn_b_out': 5.72,
     'L0_ffn_gate_w': 8.0,
     'L0_ffn_gate_bias': 8.0,
     'L0_ffn_w1': 8.0,
     'L0_ffn_w2': 8.0,
     'L0_ffn_w3': 8.0,
     'L0_ffn_sw1': 8.0,
     'L0_ffn_sw2': 8.0,
     'L0_ffn_sw3': 8.0}
    for name, (base, spread) in spreads.items():
        noise = np.random.default_rng([zlib.crc32(name.encode()), seed]).standard_normal(out[name].shape)
        drawn = base * np.exp(spread * noise) if base else spread * noise
        out[name] = jnp.asarray(drawn.astype(out[name].dtype))
    for name, factor in factors.items():
        out[name] = (out[name] * factor).astype(out[name].dtype)
    return out
```

```python
from contextlib import ExitStack

import numpy as np
import concourse.bass as bass
from concourse import mybir

F32 = mybir.dt.float32
BF16 = mybir.dt.bfloat16
I32 = mybir.dt.int32
U32 = mybir.dt.uint32
ALU = mybir.AluOpType
ACT = mybir.ActivationFunctionType
AX = mybir.AxisListType

P = 128
B, SQ, D, SK = 4, 256, 128, 512
HEADS, DH = 16, 8
GH = 4
GROUPS = HEADS // GH
STEPS = B * GROUPS
KT = SK // P
QT = SQ // P
TOK = B * SQ
TT = TOK // P
E, INTER, TOPK = 8, 256, 2
MT = INTER // P
HALF = 512
NHALF = TOK // HALF
EPS = 1e-5
MASKED = -99957650920014020608.0
SCALE = 1.0 / float(np.sqrt(DH))
LOWEST = -3.0e38
K_PARTS = [0, 0, 0, 1, 1, 2]
Q_PARTS = [0, 1, 2, 0, 1, 0]
SLOTS = len(K_PARTS)
SHIFT_ROW = 64
SUM_ROW = DH
C_ID, C_SEL, C_MEAN, C_ONE, C_LT = 0, P, 2 * P, 3 * P, 4 * P
C_W = 4 * P + E * E


def build(nc, xT, ctxT, ctx, mask, wo, gateT, gbias, ffn, cst, outT, comb, k_scr, q_scr):
    with ExitStack() as st:
        def sb(name, shape, dt=F32):
            return st.enter_context(nc.sbuf_tensor(name, shape, dt))

        def sem(name):
            return st.enter_context(nc.semaphore(name))

        cs = sb("cs", [P, C_W])
        ident = cs[:, C_ID:C_ID + P]
        sel = cs[:, C_SEL:C_SEL + P]
        mean_w = cs[:, C_MEAN:C_MEAN + P]
        ones = cs[:, C_ONE:C_ONE + P]
        lower = cs[:, C_LT:C_LT + E * E]
        identb = sb("identb", [P, 2, P], BF16)
        xt = sb("xt", [P, TOK])
        kT = sb("kT", [P, B, SK])
        vN = sb("vN", [P, B * KT, D])
        mask_i = sb("mask_i", [P, B * QT, SK], I32)
        mask_b = sb("mask_b", [P, B * QT, SK], BF16)
        wo_sb = sb("wo_sb", [P, GROUPS, D])
        gate_sb = sb("gate_sb", [P, E])
        gb_sb = sb("gb_sb", [P, E])
        k_part = sb("k_part", [P, 3, SK], BF16)
        q_part = sb("q_part", [P, 3, SQ], BF16)
        k_rest = sb("k_rest", [P, SK])
        q_rest = sb("q_rest", [P, SQ])
        k_st = [sb(f"k_st{i}", [P, HEADS, SK], BF16) for i in range(2)]
        q_st = [sb(f"q_st{i}", [P, HEADS, SQ], BF16) for i in range(2)]
        v_st = sb("v_st", [P, GROUPS, KT, GH, 32])
        junk = sb("junk", [P, QT, SK], BF16)
        rmax = sb("rmax", [P, 2, QT, GH])
        s_rest = sb("s_rest", [P, QT, GH])
        s_part = sb("s_part", [P, 2, QT, 3, GH], BF16)
        s_row = sb("s_row", [3 * GH, 2, SQ], BF16)
        prob = [sb(f"prob{i}", [P, KT, GH, SQ]) for i in range(2)]
        pv_sb = sb("pv_sb", [P, SQ])
        rsum = sb("rsum", [P, SQ])
        o_n = sb("o_n", [P, GROUPS, SQ])
        dif = [sb(f"dif{i}", [P, SQ]) for i in range(2)]
        sq = [sb(f"sq{i}", [P, SQ]) for i in range(2)]
        vareps = [sb(f"vareps{i}", [P, QT]) for i in range(2)]
        rstd = [sb(f"rstd{i}", [P, QT]) for i in range(2)]
        diag = [sb(f"diag{i}", [P, QT, P]) for i in range(2)]
        mhalf = sb("mhalf", [P, QT])
        qn = sb("qn", [P, SQ])
        x1 = sb("x1", [P, TOK])
        xn2 = sb("xn2", [P, TOK])
        lg = sb("lg", [P, TT, E])
        r1 = sb("r1", [P, TT])
        ex = sb("ex", [P, TT, E])
        scr = sb("scr", [P, TT, E])
        bia = sb("bia", [P, TT, E])
        gtm = sb("gtm", [P, TT, E, E])
        eqm = sb("eqm", [P, TT, E, E])
        rank = sb("rank", [P, TT, E])
        cw = sb("cw", [P, E, TT])
        cwT = sb("cwT", [E * TT, P])
        cb = sb("cb", [P, 2, TOK])
        w_sb = [sb(f"w_sb{i}", [P, 3 * INTER]) for i in range(2)]
        sil = [sb(f"sil{i}", [P, MT, HALF]) for i in range(2)]
        gat = [sb(f"gat{i}", [P, MT, HALF]) for i in range(2)]

        ps = st.enter_context(nc.psum_tensor("ps", [P, 8, 512], F32))
        MAXB, PVB, MISC = 4, 6, 7
        H3 = [2, 6]
        YB = 4

        cst_in, x0_in, x_in, k0_in, k_in, v_in, m0_in, m_in, wo_in, gate_in = [
            sem(n) for n in "cst_in x0_in x_in k0_in k_in v_in m0_in m_in wo_in gate_in".split()]
        k_stacked = [sem(f"k_stacked{i}") for i in range(2)]
        q_stacked = [sem(f"q_stacked{i}") for i in range(2)]
        shift_in = [sem(f"shift_in{i}") for i in range(2)]
        k_out = sem("k_out")
        q_out = sem("q_out")
        stack_zero = [sem(f"stack_zero{i}") for i in range(2)]
        ones_ok = [sem(f"ones_ok{i}") for i in range(2)]
        identb_ok = sem("identb_ok")
        v_placed = sem("v_placed")
        v_zero = sem("v_zero")
        mask_ok = sem("mask_ok")
        kp_chain = sem("kp_chain")
        kp_ok = sem("kp_ok")
        qp_chain = sem("qp_chain")
        qp_ok = sem("qp_ok")
        max_scored = sem("max_scored")
        max_taken = sem("max_taken")
        sp_chain = sem("sp_chain")
        sp_ok = sem("sp_ok")
        srow_ok = sem("srow_ok")
        scored = sem("scored")
        exp_ok = sem("exp_ok")
        pv_ok = sem("pv_ok")
        pv_copied = sem("pv_copied")
        sum_ok = sem("sum_ok")
        rsum_ok = sem("rsum_ok")
        on_ok = sem("on_ok")
        misc_written = sem("misc_written")
        misc_read = sem("misc_read")
        x1_ok = sem("x1_ok")
        dif_ok = [sem(f"dif_ok{i}") for i in range(2)]
        sq_ok = [sem(f"sq_ok{i}") for i in range(2)]
        var_ok = [sem(f"var_ok{i}") for i in range(2)]
        rstd_ok = [sem(f"rstd_ok{i}") for i in range(2)]
        diag_ok = [sem(f"diag_ok{i}") for i in range(2)]
        norm_ok = [sem(f"norm_ok{i}") for i in range(2)]
        lg_ok = sem("lg_ok")
        r_chain = sem("r_chain")
        ex_in = sem("ex_in")
        ex_ok = sem("ex_ok")
        cw_ok = sem("cw_ok")
        cwT_ps = sem("cwT_ps")
        cwT_ok = sem("cwT_ok")
        comb_out = sem("comb_out")
        cb_in = [sem(f"cb_in{i}") for i in range(2)]
        w_in = [sem(f"w_in{i}") for i in range(2)]
        h1_ok = sem("h1_ok")
        h3_ok = sem("h3_ok")
        sil_ok = sem("sil_ok")
        scaled_ok = sem("scaled_ok")
        gat_ok = sem("gat_ok")
        y_ok = sem("y_ok")
        ot_ok = sem("ot_ok")
        out_done = sem("out_done")

        def misc_ops(n, u):
            b, g = divmod(n, GROUPS)
            ops = [("shift", n + 1)] if u == 1 and n + 1 < STEPS else []
            if g == 0 and b + 1 < B:
                ops += {0: [("mean1", b + 1)], 1: [("var1", b + 1)], 3: [("bc1", b + 1)]}.get(u, [])
            if g == 0 and u == 2 and b:
                ops += [("wout", b - 1)]
            if g == 1 and b:
                ops += {0: [("mean2", b - 1)], 1: [("var2", b - 1)], 3: [("bc2", b - 1)]}.get(u, [])
            if g == 2 and u == 1 and b:
                ops += [("gate", b - 1)]
            return ops

        misc_all = [("mean1", 0), ("var1", 0), ("bc1", 0), ("shift", 0)]
        for n in range(STEPS):
            for u in range(KT):
                misc_all += misc_ops(n, u)
        misc_all += [(w, B - 1) for w in ("wout", "mean2", "var2", "bc2", "gate")]
        misc_at = {op: i for i, op in enumerate(misc_all)}

        UNITS = (E + 1) * NHALF

        block = st.enter_context(nc.Block())

        @block.sync
        def _(sp):
            sp.dma_start(xt[:, 0:SQ], xT[:, 0:SQ]).then_inc(x0_in, 16)
            sp.dma_start(cs[:], cst).then_inc(cst_in, 16)
            sp.dma_start(mask_i[:, 0:QT, :], mask[0:SQ].rearrange("(t p) k -> p t k", p=P)).then_inc(m0_in, 16)
            sp.dma_start(xt[:, SQ:], xT[:, SQ:]).then_inc(x_in, 16)

            def stack(b):
                i = b % 2
                if b >= 2:
                    sp.wait_ge(scored, KT * GROUPS * (b - 1))
                else:
                    sp.wait_ge(stack_zero[i], 2)
                sp.wait_ge(kp_ok, b + 1)
                sp.dma_start(k_scr[b].rearrange("r p k -> p r k"), k_part[:]).then_inc(k_out, 16)
                sp.wait_ge(k_out, 16 * (b + 1))
                for s, part in enumerate(K_PARTS):
                    sp.dma_start(k_st[i][DH * s:DH * s + DH, :, :],
                                 k_scr[b, part].rearrange("(h d) k -> d h k", d=DH)).then_inc(k_stacked[i], 16)
                sp.wait_ge(qp_ok, b + 1)
                sp.dma_start(q_scr[b].rearrange("r p q -> p r q"), q_part[:]).then_inc(q_out, 16)
                sp.wait_ge(q_out, 16 * (b + 1))
                for s, part in enumerate(Q_PARTS):
                    sp.dma_start(q_st[i][DH * s:DH * s + DH, :, :],
                                 q_scr[b, part].rearrange("(h d) q -> d h q", d=DH)).then_inc(q_stacked[i], 16)

            def shift(n):
                b, g = divmod(n, GROUPS)
                sp.wait_ge(srow_ok, n + 1)
                for r in range(3):
                    row = SHIFT_ROW + r
                    sp.dma_start(q_st[b % 2][row:row + 1, GH * g:GH * g + GH, :],
                                 s_row[GH * r:GH * r + GH, n % 2, :]).then_inc(shift_in[n % 2], 16)

            stack(0)
            shift(0)
            for n in range(STEPS):
                b, g = divmod(n, GROUPS)
                if g == 1 and b + 1 < B:
                    stack(b + 1)
                if n + 1 < STEPS:
                    shift(n + 1)
            for e in range(2):
                sp.dma_start(w_sb[e][:], ffn[e]).then_inc(w_in[e], 16)
            sp.wait_ge(cwT_ok, 1)
            sp.dma_start(comb.rearrange("e (t p) -> (e t) p", p=P), cwT[:]).then_inc(comb_out, 16)
            sp.wait_ge(comb_out, 16)
            for e in range(E):
                if e >= 2:
                    sp.wait_ge(scaled_ok, NHALF * (e - 1))
                sp.dma_start(cb[:, e % 2, :], comb[e:e + 1, :].broadcast_to([P, TOK])).then_inc(cb_in[e % 2], 16)
                if e + 2 < E + 1:
                    sp.wait_ge(y_ok, NHALF * (e + 1))
                    sp.dma_start(w_sb[e % 2][:], ffn[e + 2]).then_inc(w_in[e % 2], 16)
            for h in range(NHALF):
                sp.wait_ge(ot_ok, h + 1)
                sp.dma_start(outT[:, h * HALF:(h + 1) * HALF], x1[:, h * HALF:(h + 1) * HALF]).then_inc(out_done, 16)
            sp.wait_ge(out_done, 16 * NHALF)

        @block.scalar
        def _(act):
            act.dma_start(kT[:, 0, :], ctxT[0]).then_inc(k0_in, 16)
            act.dma_start(vN[:], ctx.rearrange("(t p) d -> p t d", p=P)).then_inc(v_in, 16)
            act.dma_start(kT[:, 1:, :], ctxT[1:].rearrange("b d k -> d b k")).then_inc(k_in, 16)
            act.dma_start(mask_i[:, QT:, :], mask[SQ:].rearrange("(t p) k -> p t k", p=P)).then_inc(m_in, 16)
            act.dma_start(wo_sb[:], wo).then_inc(wo_in, 16)
            act.dma_start(gate_sb[:], gateT).then_inc(gate_in, 16)
            act.dma_start(gb_sb[:], gbias.broadcast_to([P, E])).then_inc(gate_in, 16)

            def square(i, b):
                act.wait_ge(dif_ok[i], b + 1)
                nc.scalar.activation(sq[i][:], dif[i][:], ACT.Square).then_inc(sq_ok[i], 1)

            def misc16():
                return ps[0:3 * GH, MISC, 0:SQ // 2].bitcast(BF16)

            def shift_copy(n):
                act.wait_ge(misc_written, misc_at["shift", n] + 1)
                if n >= 2:
                    act.wait_ge(shift_in[n % 2], 48 * (n // 2))
                nc.scalar.copy(s_row[:, n % 2, :], misc16()).then_inc(srow_ok, 1)

            def pv_copy(n):
                act.wait_ge(pv_ok, n + 1)
                if n:
                    act.wait_ge(on_ok, n)
                nc.scalar.copy(pv_sb[:], ps[:, PVB, 0:SQ]).then_inc(pv_copied, 1)

            square(0, 0)
            shift_copy(0)
            for n in range(STEPS):
                b, g = divmod(n, GROUPS)
                for u in range(KT):
                    if u == 0 and n:
                        pv_copy(n - 1)
                    act.wait_ge(scored, KT * n + u + 1)
                    if n >= 2 and u == 0:
                        act.wait_ge(pv_ok, n - 1)
                    bank = 2 * (u % 2)
                    nc.scalar.activation(prob[n % 2][:, u].rearrange("p j q -> p (j q)"),
                                         ps[:, bank:bank + 2, :].rearrange("p a q -> p (a q)"),
                                         ACT.Exp, scale=SCALE).then_inc(exp_ok, 1)
                    for what, i in misc_ops(n, u):
                        if what == "shift":
                            shift_copy(i)
                        if what == "mean1":
                            square(0, i)
                        if what == "mean2":
                            square(1, i)
            pv_copy(STEPS - 1)
            square(1, B - 1)
            act.wait_ge(ex_in, 1)
            nc.scalar.activation(ex[:], ex[:], ACT.Exp).then_inc(ex_ok, 1)

            def silu(v):
                act.wait_ge(h1_ok, v + 1)
                if v >= 2:
                    act.wait_ge(gat_ok, v - 1)
                nc.scalar.activation(sil[v % 2][:].rearrange("p m t -> p (m t)"),
                                     ps[:, 0:MT, :].rearrange("p m t -> p (m t)"), ACT.Silu).then_inc(sil_ok, 1)

            for v in range(UNITS):
                silu(v)
                if v == 1:
                    act.wait_ge(cwT_ps, 1)
                    nc.scalar.copy(cwT[:], ps[0:E * TT, YB + 1, 0:P]).then_inc(cwT_ok, 1)

        @block.gpsimd
        def _(pool):
            nc.gpsimd.memset(k_st[0][:].bitcast(U32), 0).then_inc(stack_zero[0], 1)
            nc.gpsimd.memset(v_st[:], 0.0).then_inc(v_zero, 1)
            nc.gpsimd.memset(mhalf[:], -0.5).then_inc(v_zero, 1)
            pool.wait_ge(v_zero, 1)
            nc.gpsimd.memset(v_st[:, :, :, :, SUM_ROW:SUM_ROW + 1], 1.0).then_inc(v_zero, 1)

            def power(i, b):
                pool.wait_ge(var_ok[i], b + 1)
                nc.gpsimd.tensor_tensor(rstd[i][:], vareps[i][:], mhalf[:], ALU.pow).then_inc(rstd_ok[i], 1)

            def split_q(b):
                pool.wait_ge(norm_ok[0], b + 1)
                pool.wait_ge(q_out, 16 * b)
                nc.gpsimd.tensor_copy(q_part[:, 0, :], qn[:]).then_inc(qp_chain, 1)
                pool.wait_ge(qp_chain, 3 * b + 1)
                nc.gpsimd.tensor_tensor(q_rest[:], qn[:], q_part[:, 0, :], ALU.subtract).then_inc(qp_chain, 1)
                pool.wait_ge(qp_chain, 3 * b + 2)
                nc.gpsimd.tensor_copy(q_part[:, 1, :], q_rest[:]).then_inc(qp_chain, 1)
                pool.wait_ge(qp_chain, 3 * b + 3)
                nc.gpsimd.tensor_tensor(q_part[:, 2, :], q_rest[:], q_part[:, 1, :], ALU.subtract).then_inc(qp_ok, 1)

            def split_k(b):
                if b == 1:
                    pool.wait_ge(k_in, 16)
                pool.wait_ge(k_out, 16 * b)
                nc.gpsimd.tensor_copy(k_part[:, 0, :], kT[:, b, :]).then_inc(kp_chain, 1)
                pool.wait_ge(kp_chain, 3 * b + 1)
                nc.gpsimd.tensor_tensor(k_rest[:], kT[:, b, :], k_part[:, 0, :], ALU.subtract).then_inc(kp_chain, 1)
                pool.wait_ge(kp_chain, 3 * b + 2)
                nc.gpsimd.tensor_copy(k_part[:, 1, :], k_rest[:]).then_inc(kp_chain, 1)
                pool.wait_ge(kp_chain, 3 * b + 3)
                nc.gpsimd.tensor_tensor(k_part[:, 2, :], k_rest[:], k_part[:, 1, :], ALU.subtract).then_inc(kp_ok, 1)

            def place_v(n):
                b, g = divmod(n, GROUPS)
                if n >= GROUPS:
                    pool.wait_ge(pv_ok, n - GROUPS + 1)
                nc.gpsimd.tensor_copy(
                    v_st[:, g, :, :, 0:DH],
                    vN[:, KT * b:KT * b + KT, GH * DH * g:GH * DH * (g + 1)].rearrange("p t (j d) -> p t j d", d=DH)
                ).then_inc(v_placed, 1)

            pool.wait_ge(v_zero, 3)
            power(0, 0)
            nc.gpsimd.memset(k_st[1][:].bitcast(U32), 0).then_inc(stack_zero[1], 1)
            pool.wait_ge(stack_zero[1], 2)
            nc.gpsimd.memset(k_st[1][SHIFT_ROW:SHIFT_ROW + 3, :, :], 1.0).then_inc(ones_ok[1], 1)
            pool.wait_ge(ones_ok[1], 1)
            pool.wait_ge(v_in, 16)
            for n in range(GROUPS):
                place_v(n)
            split_k(1)
            for n in range(STEPS):
                b, g = divmod(n, GROUPS)
                for u in range(KT):
                    for what, i in misc_ops(n, u):
                        if what == "var1":
                            power(0, i)
                        if what == "bc1":
                            split_q(i)
                        if what == "var2":
                            power(1, i)
                    if u == 2 and n and n + GROUPS - 1 < STEPS:
                        place_v(n + GROUPS - 1)
                    if g == 3 and u == 2 and b + 2 < B:
                        split_k(b + 2)
            power(1, B - 1)
            for v in range(NHALF, UNITS):
                e, h = v // NHALF - 1, v % NHALF
                pool.wait_ge(cb_in[e % 2], 16 * (e // 2 + 1))
                pool.wait_ge(sil_ok, v + 1)
                s = sil[v % 2]
                nc.gpsimd.tensor_tensor(s[:], s[:], cb[:, e % 2:e % 2 + 1, h * HALF:(h + 1) * HALF].broadcast_to([P, MT, HALF]),
                                        ALU.mult).then_inc(scaled_ok, 1)

        @block.vector
        def _(dve):
            V = nc.vector
            V.memset(q_st[0][:].bitcast(U32), 0).then_inc(stack_zero[0], 1)
            V.memset(q_st[1][:].bitcast(U32), 0).then_inc(stack_zero[1], 1)
            dve.wait_ge(stack_zero[0], 2)
            V.memset(k_st[0][SHIFT_ROW:SHIFT_ROW + 3, :, :], 1.0).then_inc(ones_ok[0], 1)

            def norm_dif(i, b):
                src = (xt, x1)[i]
                dve.wait_ge(misc_written, misc_at[f"mean{i + 1}", b] + 1)
                if i == 1:
                    dve.wait_ge(x1_ok, b + 1)
                V.tensor_tensor(dif[i][:], src[:, SQ * b:SQ * (b + 1)], ps[:, MISC, 0:SQ],
                                ALU.subtract).then_inc(dif_ok[i], 1)

            def norm_var(i, b):
                dve.wait_ge(misc_written, misc_at[f"var{i + 1}", b] + 1)
                V.tensor_scalar(vareps[i][:], ps[:, MISC, 0:QT], EPS, None, ALU.add).then_inc(var_ok[i], 1)

            def norm_diag(i, b):
                dve.wait_ge(rstd_ok[i], b + 1)
                for t in range(QT):
                    ins = V.tensor_scalar(diag[i][:, t, :], ident, rstd[i][:, t:t + 1], None, ALU.mult)
                ins.then_inc(diag_ok[i], 1)

            def norm_out(i, b):
                dve.wait_ge(misc_written, misc_at[f"bc{i + 1}", b] + 1)
                if i == 0 and b:
                    dve.wait_ge(qp_ok, b)
                out = (qn[:], xn2[:, SQ * b:SQ * (b + 1)])[i]
                V.tensor_tensor(out, dif[i][:], ps[:, MISC, 0:SQ], ALU.mult).then_inc(norm_ok[i], 1)

            def masks(b):
                dve.wait_ge(m_in if b else m0_in, 16)
                V.tensor_scalar(mask_b[:, QT * b:QT * (b + 1), :], mask_i[:, QT * b:QT * (b + 1), :], 0.0, MASKED,
                                ALU.is_equal, ALU.mult).then_inc(mask_ok, 1)

            def row_max(n, j):
                b = n // GROUPS
                for t in range(QT):
                    dve.wait_ge(max_scored, QT * (GH * n + j) + t + 1)
                    V.tensor_tensor_reduce(out=junk[:, t, :], in0=ps[:, MAXB + t, :], in1=mask_b[:, QT * b + t, :],
                                           scale=1.0, scalar=LOWEST, op0=ALU.add, op1=ALU.max,
                                           accum_out=rmax[:, n % 2, t, j:j + 1]).then_inc(max_taken, 1)

            def shift_parts(n):
                i = n % 2
                dve.wait_ge(max_taken, QT * GH * (n + 1))
                if n >= 2:
                    dve.wait_ge(srow_ok, n - 1)
                V.tensor_scalar(s_part[:, i, :, 0, :], rmax[:, i], -1.0, None, ALU.mult).then_inc(sp_chain, 1)
                dve.wait_ge(sp_chain, 3 * n + 1)
                V.scalar_tensor_tensor(out=s_rest[:], in0=rmax[:, i], scalar=-1.0, in1=s_part[:, i, :, 0, :],
                                       op0=ALU.mult, op1=ALU.subtract).then_inc(sp_chain, 1)
                dve.wait_ge(sp_chain, 3 * n + 2)
                V.tensor_copy(s_part[:, i, :, 1, :], s_rest[:]).then_inc(sp_chain, 1)
                dve.wait_ge(sp_chain, 3 * n + 3)
                V.tensor_tensor(s_part[:, i, :, 2, :], s_rest[:], s_part[:, i, :, 1, :],
                                ALU.subtract).then_inc(sp_ok, 1)

            def normalize(n):
                dve.wait_ge(sum_ok, n + 1)
                V.reciprocal(rsum[:], ps[:, PVB, SQ:2 * SQ]).then_inc(rsum_ok, 1)
                dve.wait_ge(rsum_ok, n + 1)
                V.tensor_tensor(o_n[:, n % GROUPS, :], pv_sb[:], rsum[:], ALU.mult).then_inc(on_ok, 1)

            def residual(b):
                dve.wait_ge(misc_written, misc_at["wout", b] + 1)
                V.tensor_tensor(x1[:, SQ * b:SQ * (b + 1)], ps[:, MISC, 0:SQ], xt[:, SQ * b:SQ * (b + 1)],
                                ALU.add).then_inc(x1_ok, 1)

            def gate_copy(b):
                dve.wait_ge(misc_written, misc_at["gate", b] + 1)
                V.tensor_copy(lg[:, QT * b:QT * (b + 1), :],
                              ps[:, MISC, 0:QT * E].rearrange("p (t e) -> p t e", e=E)).then_inc(lg_ok, 1)

            def misc_use(what, i):
                if what in ("mean1", "mean2"):
                    norm_dif(int(what[-1]) - 1, i)
                if what in ("var1", "var2"):
                    norm_var(int(what[-1]) - 1, i)
                if what in ("bc1", "bc2"):
                    norm_out(int(what[-1]) - 1, i)
                if what == "wout":
                    residual(i)
                if what == "gate":
                    gate_copy(i)

            def split(part, rest, src, chain, done):
                V.tensor_copy(part[:, 0, :], src).then_inc(chain, 1)
                dve.wait_ge(chain, 1)
                V.tensor_tensor(rest[:], src, part[:, 0, :], ALU.subtract).then_inc(chain, 1)
                dve.wait_ge(chain, 2)
                V.tensor_copy(part[:, 1, :], rest[:]).then_inc(chain, 1)
                dve.wait_ge(chain, 3)
                V.tensor_tensor(part[:, 2, :], rest[:], part[:, 1, :], ALU.subtract).then_inc(done, 1)

            dve.wait_ge(x0_in, 16)
            norm_dif(0, 0)
            V.tensor_copy(identb[:, 0, :], ident).then_inc(identb_ok, 1)
            V.tensor_copy(identb[:, 1, :], ident).then_inc(identb_ok, 1)
            norm_var(0, 0)
            dve.wait_ge(k0_in, 16)
            split(k_part, k_rest, kT[:, 0, :], kp_chain, kp_ok)
            norm_diag(0, 0)
            norm_out(0, 0)
            dve.wait_ge(norm_ok[0], 1)
            split(q_part, q_rest, qn[:], qp_chain, qp_ok)
            masks(0)
            dve.wait_ge(mask_ok, 1)
            for n in range(2):
                for j in range(GH):
                    row_max(n, j)
                shift_parts(n)
            for n in range(STEPS):
                b, g = divmod(n, GROUPS)
                for u in range(KT):
                    if n + 2 < STEPS:
                        if u == 0 and (n + 2) % GROUPS == 0:
                            dve.wait_ge(mask_ok, (n + 2) // GROUPS + 1)
                        row_max(n + 2, u)
                    for what, i in misc_ops(n, u):
                        misc_use(what, i)
                    if u == 1 and n:
                        normalize(n - 1)
                    if u == 2:
                        if g == 0 and b + 1 < B:
                            norm_diag(0, b + 1)
                            masks(b + 1)
                        if g == 1 and b:
                            norm_diag(1, b - 1)
                    if u == 3 and n + 2 < STEPS:
                        shift_parts(n + 2)
            normalize(STEPS - 1)
            residual(B - 1)
            norm_dif(1, B - 1)
            norm_var(1, B - 1)
            norm_diag(1, B - 1)
            norm_out(1, B - 1)
            gate_copy(B - 1)

            def gate_unit(v):
                dve.wait_ge(h3_ok, v + 1)
                if v >= NHALF:
                    dve.wait_ge(scaled_ok, v - NHALF + 1)
                else:
                    dve.wait_ge(sil_ok, v + 1)
                if v >= 2:
                    dve.wait_ge(y_ok, v - 1)
                bank = H3[v % 2]
                V.tensor_tensor(gat[v % 2][:], sil[v % 2][:], ps[:, bank:bank + MT, :], ALU.mult).then_inc(gat_ok, 1)

            steps = [0]

            def link(ins):
                steps[0] += 1
                ins.then_inc(r_chain, 1)
                dve.wait_ge(r_chain, steps[0])

            dve.wait_ge(lg_ok, B)
            dve.wait_ge(gate_in, 32)
            link(V.tensor_reduce(r1[:], lg[:], AX.X, ALU.max))
            V.tensor_tensor(ex[:], lg[:], r1[:].unsqueeze(2).broadcast_to([P, TT, E]), ALU.subtract).then_inc(ex_in, 1)
            dve.wait_ge(ex_ok, 1)
            link(V.tensor_reduce(r1[:], ex[:], AX.X, ALU.add))
            link(V.reciprocal(r1[:], r1[:]))
            link(V.tensor_tensor(scr[:], ex[:], r1[:].unsqueeze(2).broadcast_to([P, TT, E]), ALU.mult))
            link(V.tensor_tensor(bia[:], scr[:], gb_sb[:].unsqueeze(1).broadcast_to([P, TT, E]), ALU.add))
            other = bia[:].unsqueeze(2).broadcast_to([P, TT, E, E])
            own = bia[:].unsqueeze(3).broadcast_to([P, TT, E, E])
            V.tensor_tensor(gtm[:], other, own, ALU.is_gt).then_inc(r_chain, 1)
            steps[0] += 1
            link(V.tensor_tensor(eqm[:], other, own, ALU.is_equal))
            link(V.tensor_tensor(eqm[:], eqm[:], lower.rearrange("p (a b) -> p a b", a=E).unsqueeze(1)
                                 .broadcast_to([P, TT, E, E]), ALU.mult))
            link(V.tensor_tensor(gtm[:], gtm[:], eqm[:], ALU.add))
            link(V.tensor_reduce(rank[:], gtm[:], AX.X, ALU.add))
            V.scalar_tensor_tensor(out=cw[:].rearrange("p e t -> p t e"), in0=rank[:], scalar=float(TOPK), in1=scr[:],
                                   op0=ALU.is_lt, op1=ALU.mult).then_inc(cw_ok, 1)
            for v in range(UNITS):
                gate_unit(v)
            for h in range(NHALF):
                dve.wait_ge(y_ok, UNITS - NHALF + h + 1)
                V.tensor_tensor(x1[:, h * HALF:(h + 1) * HALF], ps[:, YB + h, :], x1[:, h * HALF:(h + 1) * HALF],
                                ALU.add).then_inc(ot_ok, 1)

        @block.tensor
        def _(pe):
            T = nc.tensor

            def misc_start(what, i):
                k = misc_at[what, i]
                reads = {"mean1": lambda j: (dif_ok[0], j + 1), "mean2": lambda j: (dif_ok[1], j + 1),
                         "var1": lambda j: (var_ok[0], j + 1), "var2": lambda j: (var_ok[1], j + 1),
                         "bc1": lambda j: (norm_ok[0], j + 1), "bc2": lambda j: (norm_ok[1], j + 1),
                         "shift": lambda j: (srow_ok, j + 1), "wout": lambda j: (x1_ok, j + 1),
                         "gate": lambda j: (lg_ok, j + 1)}
                if k:
                    w, j = misc_all[k - 1]
                    pe.wait_ge(*reads[w](j))

            def misc_op(what, i):
                misc_start(what, i)
                out = ps[:, MISC, :]
                if what in ("mean1", "mean2"):
                    src = xt if what == "mean1" else x1
                    if what == "mean1":
                        pe.wait_ge(*((x_in, 16) if i else (x0_in, 16)))
                    else:
                        pe.wait_ge(x1_ok, i + 1)
                    ins = T.matmul(out[:, 0:SQ], mean_w, src[:, SQ * i:SQ * (i + 1)], start=True, stop=True)
                if what in ("var1", "var2"):
                    z = int(what[-1]) - 1
                    pe.wait_ge(sq_ok[z], i + 1)
                    for t in range(QT):
                        ins = T.matmul(out[:, t:t + 1], sq[z][:, P * t:P * (t + 1)], mean_w[:, 0:1], start=True, stop=True)
                if what in ("bc1", "bc2"):
                    z = int(what[-1]) - 1
                    pe.wait_ge(diag_ok[z], i + 1)
                    ins = T.matmul(out[:, 0:SQ], ones, diag[z][:].rearrange("p t q -> p (t q)"), start=True, stop=True)
                if what == "shift":
                    pe.wait_ge(sp_ok, i + 1)
                    for t in range(QT):
                        ins = T.transpose(out[0:3 * GH, P // 2 * t:P // 2 * (t + 1)].bitcast(BF16),
                                          s_part[:, i % 2, t].rearrange("p r j -> p (r j)"), identb[:, 0, :])
                if what == "wout":
                    if i == 0:
                        pe.wait_ge(wo_in, 16)
                    pe.wait_ge(on_ok, GROUPS * (i + 1))
                    for g in range(GROUPS):
                        ins = T.matmul(out[:, 0:SQ], wo_sb[:, g, :], o_n[:, g, :], start=(g == 0), stop=(g == GROUPS - 1))
                if what == "gate":
                    if i == 0:
                        pe.wait_ge(gate_in, 32)
                    pe.wait_ge(norm_ok[1], i + 1)
                    for t in range(QT):
                        ins = T.matmul(out[:, E * t:E * (t + 1)], xn2[:, SQ * i + P * t:SQ * i + P * (t + 1)], gate_sb[:],
                                       start=True, stop=True)
                ins.then_inc(misc_written, 1)

            def max_scores(n, j):
                b, g = divmod(n, GROUPS)
                if g == 0 and j == 0:
                    pe.wait_ge(ones_ok[b % 2], 1)
                    pe.wait_ge(k_stacked[b % 2], 16 * SLOTS * (b // 2 + 1))
                    pe.wait_ge(q_stacked[b % 2], 16 * SLOTS * (b // 2 + 1))
                h = GH * g + j
                for t in range(QT):
                    r = QT * (GH * n + j) + t
                    if r >= QT:
                        pe.wait_ge(max_taken, r - QT + 1)
                    T.matmul(ps[:, MAXB + t, :], q_st[b % 2][:, h, P * t:P * (t + 1)], k_st[b % 2][:, h, :],
                             start=True, stop=True).then_inc(max_scored, 1)

            def scores(n, u):
                b, g = divmod(n, GROUPS)
                if u == 0:
                    pe.wait_ge(shift_in[n % 2], 48 * (n // 2 + 1))
                if KT * n + u >= 2:
                    pe.wait_ge(exp_ok, KT * n + u - 1)
                for a in range(2):
                    out = ps[:, 2 * (u % 2) + a, :]
                    for c in range(2):
                        h = GH * g + 2 * a + c
                        T.matmul(out[:, SQ * c:SQ * (c + 1)], k_st[b % 2][:, h, P * u:P * (u + 1)], q_st[b % 2][:, h, :],
                                 start=(c == 0), stop=False, skip_group_check=True)
                    for t in range(QT):
                        ins = T.matmul(out.rearrange("p (c q) -> p c q", c=2)[:, :, P * t:P * (t + 1)],
                                       mask_b[:, QT * b + t, P * u:P * (u + 1)], identb[:],
                                       start=False, stop=(t == QT - 1), skip_group_check=True)
                ins.then_inc(scored, 1)

            def values(n):
                pe.wait_ge(exp_ok, KT * (n + 1))
                pe.wait_ge(v_placed, n + 1)
                if n:
                    pe.wait_ge(rsum_ok, n)
                for u in range(KT):
                    for j in range(GH):
                        ins = T.matmul(ps[32 * j:32 * j + 32, PVB, 0:SQ], v_st[:, n % GROUPS, u, j, :],
                                       prob[n % 2][:, u, j, :], start=(u == 0), stop=(u == KT - 1),
                                       skip_group_check=True)
                ins.then_inc(pv_ok, 1)

            def sums(n):
                pe.wait_ge(pv_copied, n + 1)
                T.matmul(ps[:, PVB, SQ:2 * SQ], sel, pv_sb[:], start=True, stop=True).then_inc(sum_ok, 1)

            pe.wait_ge(cst_in, 16)
            misc_op("mean1", 0)
            misc_op("var1", 0)
            misc_op("bc1", 0)
            pe.wait_ge(identb_ok, 2)
            for j in range(GH):
                max_scores(0, j)
            for j in range(GH):
                if j == 2:
                    misc_op("shift", 0)
                max_scores(1, j)
            pe.wait_ge(mask_ok, 1)
            for n in range(STEPS):
                for u in range(KT):
                    if u == 0 and n:
                        values(n - 1)
                    scores(n, u)
                    if n + 2 < STEPS:
                        max_scores(n + 2, u)
                    if u == 1 and n:
                        sums(n - 1)
                    for what, i in misc_ops(n, u):
                        misc_op(what, i)

            def weights(v):
                return w_sb[v // NHALF % 2]

            def h1(v):
                e, h = divmod(v, NHALF)
                if h == 0:
                    pe.wait_ge(w_in[e % 2], 16 * (e // 2 + 1))
                pe.wait_ge(*((sil_ok, v) if v else (exp_ok, KT * STEPS)))
                for m in range(MT):
                    ins = T.matmul(ps[:, m, :], weights(v)[:, P * m:P * (m + 1)], xn2[:, HALF * h:HALF * (h + 1)],
                                   start=True, stop=True)
                ins.then_inc(h1_ok, 1)

            def h3(v):
                h = v % NHALF
                if v >= 2:
                    pe.wait_ge(gat_ok, v - 1)
                for m in range(MT):
                    ins = T.matmul(ps[:, H3[v % 2] + m, :], weights(v)[:, INTER + P * m:INTER + P * (m + 1)],
                                   xn2[:, HALF * h:HALF * (h + 1)], start=True, stop=True)
                ins.then_inc(h3_ok, 1)

            def down(v):
                e, h = divmod(v, NHALF)
                pe.wait_ge(gat_ok, v + 1)
                if v == 1:
                    pe.wait_ge(cwT_ok, 1)
                for m in range(MT):
                    ins = T.matmul(ps[:, YB + h, :], weights(v)[:, 2 * INTER + P * m:2 * INTER + P * (m + 1)],
                                   gat[v % 2][:, m, :], start=(e == 0 and m == 0), stop=(e == E and m == MT - 1),
                                   skip_group_check=True)
                ins.then_inc(y_ok, 1)

            values(STEPS - 1)
            h1(0)
            sums(STEPS - 1)
            misc_op("wout", B - 1)
            h3(0)
            for what in ("mean2", "var2", "bc2", "gate"):
                misc_op(what, B - 1)
            pe.wait_ge(lg_ok, B)
            for v in range(1, UNITS + 1):
                if v < UNITS:
                    h1(v)
                    h3(v)
                if v == 2:
                    pe.wait_ge(cw_ok, 1)
                    T.transpose(ps[0:E * TT, YB + 1, 0:P], cw[:].rearrange("p e t -> p (e t)"), ident).then_inc(cwT_ps, 1)
                down(v - 1)


def kernel(**inputs):
    import concourse.bacc as _bacc
    from concourse.bass_utils import run_bass_kernel_spmd as _run

    a = {k: np.asarray(v) for k, v in inputs.items()}
    w_out, b_out = a["L0_xattn_W_out"], a["L0_xattn_b_out"]
    wo = np.zeros((GH, 32, GROUPS, D), np.float32)
    wo[:, 0:DH] = w_out.T.reshape(GROUPS, GH, DH, D).transpose(1, 2, 0, 3)
    wo[0, SUM_ROW, 0] = b_out

    def up(w, sw):
        return np.concatenate([sw[None], w]).transpose(0, 2, 1)

    def down(w, sw):
        return np.concatenate([sw[None], w]).transpose(0, 2, 1).reshape(E + 1, MT, P, D).transpose(0, 2, 1, 3).reshape(E + 1, P, MT * D)

    ffn = np.concatenate([up(a["L0_ffn_w1"], a["L0_ffn_sw1"]), up(a["L0_ffn_w3"], a["L0_ffn_sw3"]),
                          down(a["L0_ffn_w2"], a["L0_ffn_sw2"])], axis=2)
    cst = np.zeros((P, C_W), np.float32)
    cst[:, C_ID:C_ID + P] = np.eye(P)
    cst[32 * (np.arange(P) // 32) + SUM_ROW, C_SEL + np.arange(P)] = 1.0
    cst[:, C_MEAN:C_MEAN + P] = 1.0 / D
    cst[:, C_ONE:C_ONE + P] = 1.0
    cst[:, C_LT:] = np.tril(np.ones((E, E)), -1).reshape(-1)
    arrays = {
        "xT": a["x"].reshape(TOK, D).T, "ctxT": a["ctx_1024"].transpose(0, 2, 1), "ctx": a["ctx_1024"].reshape(B * SK, D),
        "mask": a["mask_Bx1xSxS2_ik1"].reshape(TOK, SK), "wo": wo.reshape(P, GROUPS, D), "gateT": a["L0_ffn_gate_w"].T,
        "gbias": a["L0_ffn_gate_bias"].reshape(1, E), "ffn": ffn, "cst": cst,
    }
    arrays = {f"in_{k}": np.ascontiguousarray(v) for k, v in arrays.items()}
    nc = _bacc.Bacc("TRN2", target_bir_lowering=False, num_devices=1)
    args = [nc.dram_tensor(k, v.shape, mybir.dt.from_np(v.dtype), kind="ExternalInput").ap() for k, v in arrays.items()]
    out = nc.dram_tensor("out_0_dram", (P, TOK), F32, kind="ExternalOutput").ap()
    comb = nc.dram_tensor("comb_dram", (E, TOK), F32, kind="Internal").ap()
    k_scr = nc.dram_tensor("k_scr", (B, 3, P, SK), BF16, kind="Internal").ap()
    q_scr = nc.dram_tensor("q_scr", (B, 3, P, SQ), BF16, kind="Internal").ap()
    build(nc, *args, out, comb, k_scr, q_scr)
    r = _run(nc, [arrays], core_ids=[0])
    got = np.asarray(r.results[0]["out_0_dram"])
    return np.ascontiguousarray(got.T).reshape(B, SQ, D)
```

```python
from contextlib import ExitStack

import numpy as np
import concourse.bass as bass
from concourse import mybir

F32 = mybir.dt.float32
BF16 = mybir.dt.bfloat16
I32 = mybir.dt.int32
U32 = mybir.dt.uint32
F32R = mybir.dt.float32r
ALU = mybir.AluOpType
ACT = mybir.ActivationFunctionType
AX = mybir.AxisListType

P = 128
B, SQ, D, SK = 4, 256, 128, 512
HEADS, DH = 16, 8
GH = 4
GROUPS = HEADS // GH
STEPS = B * GROUPS
KT = SK // P
QT = SQ // P
TOK = B * SQ
TT = TOK // P
E, INTER, TOPK = 8, 256, 2
MT = INTER // P
HALF = 512
NHALF = TOK // HALF
HT = HALF // P
EPS = 1e-5
MASKED = -99957650920014020608.0
SCALE = 1.0 / float(np.sqrt(DH))
LOWEST = -3.0e38
MINUS_ONES = 0xBF80BF80
K_PARTS = [0, 0, 0, 1, 1, 2]
Q_PARTS = [0, 1, 2, 0, 1, 0]
SLOTS = len(K_PARTS)
SHIFT_ROW = 64
SUM_ROW = DH
C_ID, C_MEAN, C_ONE, C_LT = 0, P, 2 * P, 3 * P
C_W = 3 * P + E * E


UNITS = [(0, 0), (1, 0), (0, 1), (2, 0), (1, 1), (2, 1)] + [(e, h) for e in range(3, E + 1) for h in range(NHALF)]
LAG = 2
W_SLOTS = 3


def routed(v):
    return sum(e > 0 for e, _ in UNITS[:v])


def last_unit(e):
    return max(v for v, (f, _) in enumerate(UNITS) if f == e)


def build(nc, xT, ctxT, ctx, mask, wo, bo, gateT, gbias, ffn, cst, outT, comb):
    with ExitStack() as st:
        def sb(name, shape, dt=F32):
            return st.enter_context(nc.sbuf_tensor(name, shape, dt))

        def sem(name):
            return st.enter_context(nc.semaphore(name))

        def sems(name, n=2):
            return [sem(f"{name}{i}") for i in range(n)]

        cs = sb("cs", [P, C_W])
        ident = cs[:, C_ID:C_ID + P]
        mean_w = cs[:, C_MEAN:C_MEAN + P]
        ones = cs[:, C_ONE:C_ONE + P]
        lower = cs[:, C_LT:C_LT + E * E]
        identb = sb("identb", [P, 2, P], BF16)
        xt = sb("xt", [P, TOK])
        kT = sb("kT", [P, B, SK])
        vN = sb("vN", [P, B * KT, D])
        mask_i = sb("mask_i", [P, 2 * QT, SK], I32)
        mask_b = sb("mask_b", [P, B * QT, SK], BF16)
        wo_sb = sb("wo_sb", [P, D])
        bo_sb = sb("bo_sb", [P, 1])
        gate_sb = sb("gate_sb", [P, E])
        gb_sb = sb("gb_sb", [P, E])
        k_part = sb("k_part", [P, 3, SK], BF16)
        q_part = sb("q_part", [P, 3, SQ], BF16)
        k_rest = sb("k_rest", [P, SK])
        q_rest = sb("q_rest", [P, SQ])
        k_st = [sb(f"k_st{i}", [P, HEADS, SK], BF16) for i in range(2)]
        q_st = [sb(f"q_st{i}", [P, HEADS, SQ], BF16) for i in range(2)]
        v_st = sb("v_st", [P, GROUPS, KT, GH, 32])
        junk = sb("junk", [P, QT, SK], BF16)
        rmax = sb("rmax", [P, 2, QT, GH])
        s_rest = sb("s_rest", [P, QT, GH])
        s_part = sb("s_part", [P, 2, QT, 3, GH], BF16)
        s_row = sb("s_row", [3 * GH, 2, SQ], BF16)
        prob = [sb(f"prob{i}", [P, KT, GH, SQ]) for i in range(2)]
        pv_sb = sb("pv_sb", [P, SQ])
        rsum = sb("rsum", [P, QT, GH])
        o_nat = sb("o_nat", [P, QT, HEADS, DH])
        oT = sb("oT", [P, SQ])
        dif = [sb(f"dif{i}", [P, SQ]) for i in range(2)]
        sq = [sb(f"sq{i}", [P, SQ]) for i in range(2)]
        vareps = [sb(f"vareps{i}", [P, QT]) for i in range(2)]
        rstd = [sb(f"rstd{i}", [P, QT]) for i in range(2)]
        diag = [sb(f"diag{i}", [P, QT, P]) for i in range(2)]
        mhalf = sb("mhalf", [P, QT])
        qn = sb("qn", [P, SQ])
        x1 = sb("x1", [P, TOK])
        xn2 = sb("xn2", [P, TOK])
        xn2_p = [sb(f"xn2_p{i}", [P, TOK], F32R) for i in range(2)]
        lg = sb("lg", [P, TT, E])
        r1 = sb("r1", [P, HT])
        ex = sb("ex", [P, HT, E])
        scr = sb("scr", [P, HT, E])
        bia = sb("bia", [P, HT, E])
        gtm = sb("gtm", [P, HT, E, E])
        eqm = sb("eqm", [P, HT, E, E])
        rank = sb("rank", [P, HT, E])
        cw = sb("cw", [P, E, HT])
        cwT = sb("cwT", [E * HT, P])
        w_raw = [sb(f"w_raw{i}", [P, 3 * INTER]) for i in range(2)]
        w_p = [[sb(f"w_p{i}_{r}", [P, 3 * INTER], F32R) for r in range(2)] for i in range(W_SLOTS)]
        g_p = [[sb(f"g_p{i}_{r}", [P, MT, HALF], F32R) for r in range(2)] for i in range(2)]

        def reuse(i):
            return prob[0][:, i].rearrange("p j q -> p (j q)")

        sil = [reuse(0), reuse(1)]
        gat = [reuse(2), reuse(3)]
        cb = [prob[1][:, i, 0:HALF // SQ].rearrange("p j q -> p (j q)") for i in range(3)]

        ps = st.enter_context(nc.psum_tensor("ps", [P, 8, 512], F32))
        MAXB, PVB, MISC = 4, 6, 7
        H3 = [2, 4]
        YB = 6

        cst_in, x0_in, x_in, k0_in, k_in, v_in, m0_in, m_in, wo_in, gate_in = [
            sem(n) for n in "cst_in x0_in x_in k0_in k_in v_in m0_in m_in wo_in gate_in".split()]
        m3_in = sem("m3_in")
        k_stacked, q_stacked, shift_in = sems("k_stacked"), sems("q_stacked"), sems("shift_in")
        stack_zero, ones_ok = sems("stack_zero"), sems("ones_ok")
        identb_ok, v_placed, v_zero, mask_ok = sem("identb_ok"), sem("v_placed"), sem("v_zero"), sem("mask_ok")
        kp_chain, kp_ok, qp_chain, qp_ok = sem("kp_chain"), sem("kp_ok"), sem("qp_chain"), sem("qp_ok")
        max_scored, max_taken = sem("max_scored"), sem("max_taken")
        sp_chain, sp_ok, srow_ok = sem("sp_chain"), sem("sp_ok"), sem("srow_ok")
        scored, exp_ok = sem("scored"), sem("exp_ok")
        pv_ok, pv_copied, pvt_ok, rsum_ok, on_ok = sem("pv_ok"), sem("pv_copied"), sem("pvt_ok"), sem("rsum_ok"), sem("on_ok")
        misc_written, oT_ok, x1_ok = sem("misc_written"), sem("oT_ok"), sem("x1_ok")
        dif_ok, sq_ok, var_ok = sems("dif_ok"), sems("sq_ok"), sems("var_ok")
        rstd_ok, diag_ok, norm_ok = sems("rstd_ok"), sems("diag_ok"), sems("norm_ok")
        xh_ok, xl_ok = sem("xh_ok"), sem("xl_ok")
        lg_ok, r_chain, ex_in, ex_ok, cw_ok, cwT_ok = (
            sem("lg_ok"), sem("r_chain"), sem("ex_in"), sem("ex_ok"), sem("cw_ok"), sem("cwT_ok"))
        comb_out = sem("comb_out")
        cb_in = sems("cb_in", 3)
        w_in = sems("w_in")
        wh_ok, wl_ok = sem("wh_ok"), sem("wl_ok")
        h1_ok, h3_ok, sil_ok, scaled_ok = sem("h1_ok"), sem("h3_ok"), sem("sil_ok"), sem("scaled_ok")
        gat_ok, gh_ok, gl_ok, y_ok, ot_ok, out_done = (
            sem("gat_ok"), sem("gh_ok"), sem("gl_ok"), sem("y_ok"), sem("ot_ok"), sem("out_done"))

        def misc_ops(n, u, place):
            b, g = divmod(n, GROUPS)
            at = (g, u, place)
            ops = []
            if (u, place) == (1, "a") and n + 1 < STEPS:
                ops.append(("shift", n + 1))
            if b + 1 < B:
                ops += {(0, 0, "b"): [("mean1", b + 1)], (0, 2, "a"): [("var1", b + 1)],
                        (0, 3, "b"): [("bc1", b + 1)]}.get(at, [])
            if b:
                ops += {(0, 2, "b"): [("oT", b - 1)], (1, 0, "a"): [("wout", b - 1)], (1, 2, "a"): [("mean2", b - 1)],
                        (1, 3, "a"): [("var2", b - 1)], (2, 0, "b"): [("bc2", b - 1)],
                        (2, 2, "a"): [("gate", b - 1)]}.get(at, [])
            if (n, u, place) == CWT0:
                ops.append(("cwT", 0))
            return ops

        ROUTE0 = (GROUPS * 2 + 3, 0)
        CWT0 = (GROUPS * 3, 0, "b")
        SPLIT_AT = [(6, 2), (7, 0), (14, 0)]
        misc_all = [("mean1", 0), ("var1", 0), ("bc1", 0), ("shift", 0)]
        for n in range(STEPS):
            for u in range(KT):
                misc_all += misc_ops(n, u, "a") + misc_ops(n, u, "b")
        misc_all += [(w, B - 1) for w in ("oT", "wout", "mean2", "var2", "bc2", "gate")] + [("cwT", 1)]
        misc_at = {op: i for i, op in enumerate(misc_all)}

        block = st.enter_context(nc.Block())

        @block.sync
        def _(sp):
            sp.dma_start(xt[:, 0:SQ], xT[:, 0:SQ]).then_inc(x0_in, 16)
            sp.dma_start(cs[:], cst).then_inc(cst_in, 16)
            sp.dma_start(mask_i[:, 0:QT, :], mask[0:SQ].rearrange("(t p) k -> p t k", p=P)).then_inc(m0_in, 16)

            def stack(b):
                i = b % 2
                if b >= 2:
                    sp.wait_ge(scored, KT * GROUPS * (b - 1))
                else:
                    sp.wait_ge(stack_zero[i], 2)
                sp.wait_ge(kp_ok, b + 1)
                for s, part in enumerate(K_PARTS):
                    sp.dma_start(k_st[i][DH * s:DH * s + DH, :, :], k_part[:, part, :]).then_inc(k_stacked[i], 16)
                sp.wait_ge(qp_ok, b + 1)
                for s, part in enumerate(Q_PARTS):
                    sp.dma_start(q_st[i][DH * s:DH * s + DH, :, :], q_part[:, part, :]).then_inc(q_stacked[i], 16)

            stack(0)
            sp.dma_start(xt[:, SQ:], xT[:, SQ:]).then_inc(x_in, 16)
            sp.dma_start(mask_i[:, QT:, :], mask[SQ:2 * SQ].rearrange("(t p) k -> p t k", p=P)).then_inc(m_in, 16)
            for e in range(2):
                sp.dma_start(w_raw[e][:], ffn[e]).then_inc(w_in[e], 16)
            for b in range(1, B):
                stack(b)
                if b + 1 < B:
                    sp.wait_ge(mask_ok, b)
                    i = (b + 1) % 2
                    sp.dma_start(mask_i[:, QT * i:QT * (i + 1), :],
                                 mask[SQ * (b + 1):SQ * (b + 2)].rearrange("(t p) k -> p t k", p=P)
                                 ).then_inc((m0_in, m_in)[i], 16)

            def load_w(e):
                sp.wait_ge(wl_ok, e - 1)
                sp.dma_start(w_raw[e % 2][:], ffn[e]).then_inc(w_in[e % 2], 16)

            def load_cb(v):
                e, h = UNITS[v]
                k = routed(v)
                if k >= 3:
                    sp.wait_ge(scaled_ok, k - 2)
                sp.dma_start(cb[k % 3], comb[e - 1:e, HALF * h:HALF * (h + 1)].broadcast_to([P, HALF])
                             ).then_inc(cb_in[k % 3], 16)

            def store_comb(h):
                sp.wait_ge(cwT_ok, h + 1)
                sp.dma_start(comb[:, HALF * h:HALF * (h + 1)].rearrange("e (t p) -> e t p", p=P), cwT[:]
                             ).then_inc(comb_out, 16)
                sp.wait_ge(comb_out, 16 * (h + 1))

            load_w(2)
            store_comb(0)
            load_w(3)
            sp.wait_ge(pv_ok, STEPS)
            load_cb(1)
            load_cb(3)
            store_comb(1)
            for v in range(4, len(UNITS)):
                load_cb(v)
                if v % 2 == 0 and (v + 4) // 2 <= E:
                    load_w((v + 4) // 2)
            for h in range(NHALF):
                sp.wait_ge(ot_ok, h + 1)
                sp.dma_start(outT[:, h * HALF:(h + 1) * HALF], x1[:, h * HALF:(h + 1) * HALF]).then_inc(out_done, 16)
            sp.wait_ge(out_done, 16 * NHALF)

        @block.scalar
        def _(act):
            act.dma_start(kT[:, 0, :], ctxT[0]).then_inc(k0_in, 16)
            for first in (x0_in, cst_in, k0_in, m0_in):
                act.wait_ge(first, 16)
            act.dma_start(vN[:], ctx.rearrange("(t p) d -> p t d", p=P)).then_inc(v_in, 16)
            act.dma_start(kT[:, 1:, :], ctxT[1:].rearrange("b d k -> d b k")).then_inc(k_in, 16)
            act.dma_start(wo_sb[:], wo).then_inc(wo_in, 16)
            act.dma_start(bo_sb[:], bo).then_inc(wo_in, 16)
            act.dma_start(gate_sb[:], gateT).then_inc(gate_in, 16)
            act.dma_start(gb_sb[:], gbias.broadcast_to([P, E])).then_inc(gate_in, 16)

            def square(i, b):
                act.wait_ge(dif_ok[i], b + 1)
                nc.scalar.activation(sq[i][:], dif[i][:], ACT.Square).then_inc(sq_ok[i], 1)

            def shift_row(n):
                b, g = divmod(n, GROUPS)
                act.wait_ge(misc_written, misc_at["shift", n] + 1)
                if n >= 2:
                    act.wait_ge(shift_in[n % 2], 16 * (n // 2))
                nc.scalar.copy(s_row[:, n % 2, :], ps[0:3 * GH, MISC, 0:SQ // 2].bitcast(BF16)).then_inc(srow_ok, 1)
                act.wait_ge(srow_ok, n + 1)
                if g == 0 and b >= 2:
                    act.wait_ge(scored, KT * GROUPS * (b - 1))
                if n == 0:
                    act.wait_ge(stack_zero[0], 2)
                if n == GROUPS:
                    act.wait_ge(stack_zero[1], 2)
                act.dma_start(q_st[b % 2][SHIFT_ROW:SHIFT_ROW + 3, GH * g:GH * g + GH, :], s_row[:, n % 2, :]
                              ).then_inc(shift_in[n % 2], 16)

            def pv_copy(n):
                act.wait_ge(pv_ok, n + 1)
                if n:
                    act.wait_ge(pvt_ok, n)
                nc.scalar.copy(pv_sb[:], ps[:, PVB, 0:SQ]).then_inc(pv_copied, 1)

            def oT_copy(b):
                act.wait_ge(misc_written, misc_at["oT", b] + 1)
                nc.scalar.copy(oT[:], ps[:, MISC, 0:SQ]).then_inc(oT_ok, 1)

            def cwT_copy(h):
                act.wait_ge(misc_written, misc_at["cwT", h] + 1)
                if h:
                    act.wait_ge(comb_out, 16 * h)
                nc.scalar.copy(cwT[:], ps[0:E * HT, MISC, 0:P]).then_inc(cwT_ok, 1)

            def route_exp(h):
                act.wait_ge(ex_in, h + 1)
                nc.scalar.activation(ex[:], ex[:], ACT.Exp).then_inc(ex_ok, 1)

            def x_high(b):
                act.wait_ge(norm_ok[1], b + 1)
                c = slice(SQ * b, SQ * (b + 1))
                nc.scalar.copy(xn2_p[0][:, c], xn2[:, c]).then_inc(xh_ok, 1)

            def w_high(e):
                act.wait_ge(w_in[e % 2], 16 * (e // 2 + 1))
                if e >= W_SLOTS:
                    act.wait_ge(y_ok, last_unit(e - W_SLOTS) + 1)
                nc.scalar.copy(w_p[e % W_SLOTS][0][:], w_raw[e % 2][:]).then_inc(wh_ok, 1)

            def misc_use(what, i):
                if what == "shift":
                    shift_row(i)
                if what == "mean1":
                    square(0, i)
                if what == "mean2":
                    square(1, i)
                if what == "oT":
                    oT_copy(i)
                if what == "cwT":
                    cwT_copy(i)

            square(0, 0)
            shift_row(0)
            for n in range(STEPS):
                for u in range(KT):
                    for op in misc_ops(n, u, "a"):
                        if op[0] != "mean2":
                            misc_use(*op)
                    act.wait_ge(scored, KT * n + u + 1)
                    if n >= 2 and u == 0:
                        act.wait_ge(pv_ok, n - 1)
                    bank = 2 * (u % 2)
                    nc.scalar.activation(prob[n % 2][:, u].rearrange("p j q -> p (j q)"),
                                         ps[:, bank:bank + 2, :].rearrange("p a q -> p (a q)"),
                                         ACT.Exp, scale=SCALE).then_inc(exp_ok, 1)
                    if u == 0 and n:
                        pv_copy(n - 1)
                    for op in misc_ops(n, u, "a"):
                        if op[0] == "mean2":
                            misc_use(*op)
                    for op in misc_ops(n, u, "b"):
                        misc_use(*op)
                    if (n, u) == ROUTE0:
                        route_exp(0)
                    if (n, u) in SPLIT_AT:
                        w_high(SPLIT_AT.index((n, u)))

            def silu(v):
                act.wait_ge(h1_ok, v + 1)
                if v >= 2:
                    act.wait_ge(gat_ok, v - 1)
                nc.scalar.activation(sil[v % 2], ps[:, 0:MT, :].rearrange("p m t -> p (m t)"),
                                     ACT.Silu).then_inc(sil_ok, 1)

            def gate_high(v):
                act.wait_ge(gat_ok, v + 1)
                if v >= 2:
                    act.wait_ge(y_ok, v - 1)
                nc.scalar.copy(g_p[v % 2][0][:].rearrange("p m t -> p (m t)"), gat[v % 2]).then_inc(gh_ok, 1)

            pv_copy(STEPS - 1)
            silu(0)
            oT_copy(B - 1)
            silu(1)
            gate_high(0)
            square(1, B - 1)
            x_high(B - 1)
            gate_high(1)
            route_exp(1)
            for v in range(2, len(UNITS)):
                silu(v)
                if v == 2:
                    cwT_copy(1)
                if v > 2:
                    gate_high(v - 1)
                if v % 2 == 0 and v >= 4 and (v + 2) // 2 <= E:
                    w_high((v + 2) // 2)
            gate_high(len(UNITS) - 1)

        @block.gpsimd
        def _(pool):
            G = nc.gpsimd
            G.memset(mhalf[:], -0.5).then_inc(v_zero, 1)
            G.memset(k_st[0][:].bitcast(U32), 0).then_inc(stack_zero[0], 1)
            pool.wait_ge(stack_zero[0], 2)
            G.memset(k_st[0][SHIFT_ROW:SHIFT_ROW + 3, :, :].bitcast(U32), MINUS_ONES).then_inc(ones_ok[0], 1)
            pool.wait_ge(ones_ok[0], 1)
            pool.wait_ge(v_zero, 1)

            def power(i, b):
                pool.wait_ge(var_ok[i], b + 1)
                G.tensor_tensor(rstd[i][:], vareps[i][:], mhalf[:], ALU.pow).then_inc(rstd_ok[i], 1)

            def split_q(b):
                pool.wait_ge(norm_ok[0], b + 1)
                pool.wait_ge(q_stacked[(b - 1) % 2], 16 * SLOTS * ((b - 1) // 2 + 1))
                G.tensor_copy(q_part[:, 0, :], qn[:]).then_inc(qp_chain, 1)
                pool.wait_ge(qp_chain, 3 * b + 1)
                G.tensor_tensor(q_rest[:], qn[:], q_part[:, 0, :], ALU.subtract).then_inc(qp_chain, 1)
                pool.wait_ge(qp_chain, 3 * b + 2)
                G.tensor_copy(q_part[:, 1, :], q_rest[:]).then_inc(qp_chain, 1)
                pool.wait_ge(qp_chain, 3 * b + 3)
                G.tensor_tensor(q_part[:, 2, :], q_rest[:], q_part[:, 1, :], ALU.subtract).then_inc(qp_ok, 1)

            def split_k(b):
                if b == 1:
                    pool.wait_ge(k_in, 16)
                pool.wait_ge(k_stacked[(b - 1) % 2], 16 * SLOTS * ((b - 1) // 2 + 1))
                G.tensor_copy(k_part[:, 0, :], kT[:, b, :]).then_inc(kp_chain, 1)
                pool.wait_ge(kp_chain, 3 * b + 1)
                G.tensor_tensor(k_rest[:], kT[:, b, :], k_part[:, 0, :], ALU.subtract).then_inc(kp_chain, 1)
                pool.wait_ge(kp_chain, 3 * b + 2)
                G.tensor_copy(k_part[:, 1, :], k_rest[:]).then_inc(kp_chain, 1)
                pool.wait_ge(kp_chain, 3 * b + 3)
                G.tensor_tensor(k_part[:, 2, :], k_rest[:], k_part[:, 1, :], ALU.subtract).then_inc(kp_ok, 1)

            def shift_parts(n):
                i = n % 2
                pool.wait_ge(max_taken, QT * GH * (n + 1))
                if n >= 2:
                    pool.wait_ge(srow_ok, n - 1)
                G.tensor_copy(s_part[:, i, :, 0, :], rmax[:, i]).then_inc(sp_chain, 1)
                pool.wait_ge(sp_chain, 3 * n + 1)
                G.tensor_tensor(s_rest[:], rmax[:, i], s_part[:, i, :, 0, :], ALU.subtract).then_inc(sp_chain, 1)
                pool.wait_ge(sp_chain, 3 * n + 2)
                G.tensor_copy(s_part[:, i, :, 1, :], s_rest[:]).then_inc(sp_chain, 1)
                pool.wait_ge(sp_chain, 3 * n + 3)
                G.tensor_tensor(s_part[:, i, :, 2, :], s_rest[:], s_part[:, i, :, 1, :],
                                ALU.subtract).then_inc(sp_ok, 1)

            def place_v(n):
                b, g = divmod(n, GROUPS)
                if n >= GROUPS:
                    pool.wait_ge(pv_ok, n - GROUPS + 1)
                G.tensor_copy(
                    v_st[:, g, :, :, 0:DH],
                    vN[:, KT * b:KT * b + KT, GH * DH * g:GH * DH * (g + 1)].rearrange("p t (j d) -> p t j d", d=DH)
                ).then_inc(v_placed, 1)

            def split_x(b):
                pool.wait_ge(norm_ok[1], b + 1)
                c = slice(SQ * b, SQ * (b + 1))
                G.tensor_copy(xn2_p[0][:, c], xn2[:, c]).then_inc(xh_ok, 1)
                pool.wait_ge(xh_ok, b + 1)
                G.tensor_tensor(xn2_p[1][:, c], xn2[:, c], xn2_p[0][:, c].bitcast(F32), ALU.subtract).then_inc(xl_ok, 1)

            def w_low(e):
                pool.wait_ge(wh_ok, e + 1)
                i = e % W_SLOTS
                G.tensor_tensor(w_p[i][1][:], w_raw[e % 2][:], w_p[i][0][:].bitcast(F32), ALU.subtract).then_inc(wl_ok, 1)

            power(0, 0)
            G.memset(v_st[:], 0.0).then_inc(v_zero, 1)
            pool.wait_ge(v_zero, 2)
            G.memset(v_st[:, :, :, :, SUM_ROW:SUM_ROW + 1], 1.0).then_inc(v_zero, 1)
            G.memset(k_st[1][:].bitcast(U32), 0).then_inc(stack_zero[1], 1)
            pool.wait_ge(stack_zero[1], 2)
            G.memset(k_st[1][SHIFT_ROW:SHIFT_ROW + 3, :, :].bitcast(U32), MINUS_ONES).then_inc(ones_ok[1], 1)
            pool.wait_ge(ones_ok[1], 1)
            pool.wait_ge(v_zero, 3)
            shift_parts(0)
            pool.wait_ge(v_in, 16)
            for n in range(GROUPS):
                place_v(n)
            split_k(1)
            shift_parts(1)
            for n in range(STEPS):
                b, g = divmod(n, GROUPS)
                for u in range(KT):
                    for what, i in misc_ops(n, u, "a"):
                        if what == "var1":
                            power(0, i)
                        if what == "var2":
                            power(1, i)
                    if u == 3 and n + 2 < STEPS:
                        shift_parts(n + 2)
                    for what, i in misc_ops(n, u, "b"):
                        if what == "bc1":
                            split_q(i)
                        if what == "bc2":
                            split_x(i)
                    if u == 2 and n and n + GROUPS - 1 < STEPS:
                        place_v(n + GROUPS - 1)
                    if g == 3 and u == 3 and b + 2 < B:
                        split_k(b + 2)
                    if (n, u) in SPLIT_AT:
                        w_low(SPLIT_AT.index((n, u)))

            def scale(v):
                k = routed(v)
                pool.wait_ge(cb_in[k % 3], 16 * (k // 3 + 1))
                pool.wait_ge(sil_ok, v + 1)
                s = sil[v % 2].rearrange("p (m t) -> p m t", m=MT)
                G.tensor_tensor(s, s, cb[k % 3].unsqueeze(1).broadcast_to([P, MT, HALF]), ALU.mult
                                ).then_inc(scaled_ok, 1)

            scale(1)
            power(1, B - 1)
            for v in range(3, len(UNITS)):
                scale(v)
                if v % 2 == 0 and v >= 4 and (v + 2) // 2 <= E:
                    w_low((v + 2) // 2)

        @block.vector
        def _(dve):
            V = nc.vector

            def norm_dif(i, b):
                src = (xt, x1)[i]
                dve.wait_ge(misc_written, misc_at[f"mean{i + 1}", b] + 1)
                if i == 1:
                    dve.wait_ge(x1_ok, b + 1)
                V.tensor_tensor(dif[i][:], src[:, SQ * b:SQ * (b + 1)], ps[:, MISC, 0:SQ],
                                ALU.subtract).then_inc(dif_ok[i], 1)

            def norm_var(i, b):
                dve.wait_ge(misc_written, misc_at[f"var{i + 1}", b] + 1)
                V.tensor_scalar(vareps[i][:], ps[:, MISC, 0:QT], EPS, None, ALU.add).then_inc(var_ok[i], 1)

            def norm_diag(i, b):
                dve.wait_ge(rstd_ok[i], b + 1)
                for t in range(QT):
                    ins = V.tensor_scalar(diag[i][:, t, :], ident, rstd[i][:, t:t + 1], None, ALU.mult)
                ins.then_inc(diag_ok[i], 1)

            def norm_out(i, b):
                dve.wait_ge(misc_written, misc_at[f"bc{i + 1}", b] + 1)
                if i == 0 and b:
                    dve.wait_ge(qp_ok, b)
                out = (qn[:], xn2[:, SQ * b:SQ * (b + 1)])[i]
                V.tensor_tensor(out, dif[i][:], ps[:, MISC, 0:SQ], ALU.mult).then_inc(norm_ok[i], 1)

            def masks(b):
                dve.wait_ge((m0_in, m_in)[b % 2], 16 * (b // 2 + 1))
                i = b % 2
                V.tensor_scalar(mask_b[:, QT * b:QT * (b + 1), :], mask_i[:, QT * i:QT * (i + 1), :], 0.0, MASKED,
                                ALU.is_equal, ALU.mult).then_inc(mask_ok, 1)

            def row_max(n, j):
                b = n // GROUPS
                if n >= 2 and j == 0:
                    dve.wait_ge(sp_ok, n - 1)
                for t in range(QT):
                    dve.wait_ge(max_scored, QT * (GH * n + j) + t + 1)
                    V.tensor_tensor_reduce(out=junk[:, t, :], in0=ps[:, MAXB + t, :], in1=mask_b[:, QT * b + t, :],
                                           scale=1.0, scalar=LOWEST, op0=ALU.add, op1=ALU.max,
                                           accum_out=rmax[:, n % 2, t, j:j + 1]).then_inc(max_taken, 1)

            def normalize(n):
                b, g = divmod(n, GROUPS)
                dve.wait_ge(pvt_ok, n + 1)
                o = ps[:, PVB, SQ:2 * SQ].rearrange("p (t j d) -> p t j d", t=QT, j=GH)
                V.reciprocal(rsum[:], o[:, :, :, SUM_ROW]).then_inc(rsum_ok, 1)
                dve.wait_ge(rsum_ok, n + 1)
                if g == 0 and b:
                    dve.wait_ge(misc_written, misc_at["oT", b - 1] + 1)
                V.tensor_tensor(o_nat[:, :, GH * g:GH * (g + 1), :], o[:, :, :, 0:DH],
                                rsum[:].unsqueeze(3).broadcast_to([P, QT, GH, DH]), ALU.mult).then_inc(on_ok, 1)

            def residual(b):
                dve.wait_ge(misc_written, misc_at["wout", b] + 1)
                if b == 0:
                    dve.wait_ge(wo_in, 32)
                V.scalar_tensor_tensor(out=x1[:, SQ * b:SQ * (b + 1)], in0=ps[:, MISC, 0:SQ], scalar=bo_sb[:, 0:1],
                                       in1=xt[:, SQ * b:SQ * (b + 1)], op0=ALU.add, op1=ALU.add).then_inc(x1_ok, 1)

            def gate_copy(b):
                dve.wait_ge(misc_written, misc_at["gate", b] + 1)
                V.tensor_copy(lg[:, QT * b:QT * (b + 1), :],
                              ps[:, MISC, 0:QT * E].rearrange("p (t e) -> p t e", e=E)).then_inc(lg_ok, 1)

            def misc_use(what, i):
                if what in ("mean1", "mean2"):
                    norm_dif(int(what[-1]) - 1, i)
                if what in ("var1", "var2"):
                    norm_var(int(what[-1]) - 1, i)
                if what in ("bc1", "bc2"):
                    norm_out(int(what[-1]) - 1, i)
                if what == "wout":
                    residual(i)
                if what == "gate":
                    gate_copy(i)

            def split(part, rest, src, chain, done):
                V.tensor_copy(part[:, 0, :], src).then_inc(chain, 1)
                dve.wait_ge(chain, 1)
                V.tensor_tensor(rest[:], src, part[:, 0, :], ALU.subtract).then_inc(chain, 1)
                dve.wait_ge(chain, 2)
                V.tensor_copy(part[:, 1, :], rest[:]).then_inc(chain, 1)
                dve.wait_ge(chain, 3)
                V.tensor_tensor(part[:, 2, :], rest[:], part[:, 1, :], ALU.subtract).then_inc(done, 1)

            steps = [0]

            def link(ins):
                steps[0] += 1
                ins.then_inc(r_chain, 1)
                dve.wait_ge(r_chain, steps[0])

            def route_scores(h):
                dve.wait_ge(lg_ok, 2 * (h + 1))
                l = lg[:, HT * h:HT * (h + 1), :]
                link(V.tensor_reduce(r1[:], l, AX.X, ALU.max))
                V.tensor_tensor(ex[:], l, r1[:].unsqueeze(2).broadcast_to([P, HT, E]), ALU.subtract).then_inc(ex_in, 1)

            def route_weights(h):
                dve.wait_ge(ex_ok, h + 1)
                if h == 0:
                    dve.wait_ge(gate_in, 32)
                link(V.tensor_reduce(r1[:], ex[:], AX.X, ALU.add))
                link(V.reciprocal(r1[:], r1[:]))
                link(V.tensor_tensor(scr[:], ex[:], r1[:].unsqueeze(2).broadcast_to([P, HT, E]), ALU.mult))
                link(V.tensor_tensor(bia[:], scr[:], gb_sb[:].unsqueeze(1).broadcast_to([P, HT, E]), ALU.add))
                other = bia[:].unsqueeze(2).broadcast_to([P, HT, E, E])
                own = bia[:].unsqueeze(3).broadcast_to([P, HT, E, E])
                V.tensor_tensor(gtm[:], other, own, ALU.is_gt).then_inc(r_chain, 1)
                steps[0] += 1
                link(V.tensor_tensor(eqm[:], other, own, ALU.is_equal))
                link(V.tensor_tensor(eqm[:], eqm[:], lower.rearrange("p (a b) -> p a b", a=E).unsqueeze(1)
                                     .broadcast_to([P, HT, E, E]), ALU.mult))
                link(V.tensor_tensor(gtm[:], gtm[:], eqm[:], ALU.add))
                link(V.tensor_reduce(rank[:], gtm[:], AX.X, ALU.add))
                if h:
                    dve.wait_ge(misc_written, misc_at["cwT", h - 1] + 1)
                V.scalar_tensor_tensor(out=cw[:].rearrange("p e t -> p t e"), in0=rank[:], scalar=float(TOPK),
                                       in1=scr[:], op0=ALU.is_lt, op1=ALU.mult).then_inc(cw_ok, 1)

            for i in range(2):
                V.memset(q_st[i][:].bitcast(U32), 0).then_inc(stack_zero[i], 1)
            dve.wait_ge(x0_in, 16)
            norm_dif(0, 0)
            dve.wait_ge(k0_in, 16)
            V.tensor_copy(k_part[:, 0, :], kT[:, 0, :]).then_inc(kp_chain, 1)
            dve.wait_ge(kp_chain, 1)
            V.tensor_tensor(k_rest[:], kT[:, 0, :], k_part[:, 0, :], ALU.subtract).then_inc(kp_chain, 1)
            V.tensor_copy(identb[:, 0, :], ident).then_inc(identb_ok, 1)
            V.tensor_copy(identb[:, 1, :], ident).then_inc(identb_ok, 1)
            norm_var(0, 0)
            dve.wait_ge(kp_chain, 2)
            V.tensor_copy(k_part[:, 1, :], k_rest[:]).then_inc(kp_chain, 1)
            dve.wait_ge(kp_chain, 3)
            V.tensor_tensor(k_part[:, 2, :], k_rest[:], k_part[:, 1, :], ALU.subtract).then_inc(kp_ok, 1)
            norm_diag(0, 0)
            masks(0)
            norm_out(0, 0)
            dve.wait_ge(norm_ok[0], 1)
            split(q_part, q_rest, qn[:], qp_chain, qp_ok)
            dve.wait_ge(mask_ok, 1)
            for n in range(2):
                for j in range(GH):
                    row_max(n, j)
            for n in range(STEPS):
                b, g = divmod(n, GROUPS)
                for u in range(KT):
                    for op in misc_ops(n, u, "a"):
                        misc_use(*op)
                    if u == 2 and n:
                        normalize(n - 1)
                    if n + 2 < STEPS:
                        if u == 0 and (n + 2) % GROUPS == 0:
                            dve.wait_ge(mask_ok, (n + 2) // GROUPS + 1)
                        row_max(n + 2, u)
                    for op in misc_ops(n, u, "b"):
                        misc_use(*op)
                        if op[0] == "mean1":
                            masks(b + 1)
                    if (g, u) == (0, 2) and b + 1 < B:
                        norm_diag(0, b + 1)
                    if (g, u) == (1, 3) and b:
                        norm_diag(1, b - 1)
                    if (n, u) == ROUTE0:
                        route_scores(0)
                    if (n, u) == (ROUTE0[0], ROUTE0[1] + 1):
                        route_weights(0)
            normalize(STEPS - 1)

            def gate_unit(v):
                dve.wait_ge(h3_ok, v + 1)
                if UNITS[v][0]:
                    dve.wait_ge(scaled_ok, routed(v + 1))
                else:
                    dve.wait_ge(sil_ok, v + 1)
                if v >= 2:
                    dve.wait_ge(gl_ok, v - 1)
                bank = H3[v % 2]
                V.tensor_tensor(gat[v % 2], sil[v % 2], ps[:, bank:bank + MT, :].rearrange("p m t -> p (m t)"),
                                ALU.mult).then_inc(gat_ok, 1)

            def gate_low(v):
                dve.wait_ge(gh_ok, v + 1)
                V.tensor_tensor(g_p[v % 2][1][:].rearrange("p m t -> p (m t)"), gat[v % 2],
                                g_p[v % 2][0][:].bitcast(F32).rearrange("p m t -> p (m t)"),
                                ALU.subtract).then_inc(gl_ok, 1)

            gate_unit(0)
            residual(B - 1)
            gate_low(0)
            norm_dif(1, B - 1)
            norm_var(1, B - 1)
            gate_unit(1)
            norm_diag(1, B - 1)
            norm_out(1, B - 1)
            c = slice(SQ * (B - 1), SQ * B)
            dve.wait_ge(xh_ok, B)
            V.tensor_tensor(xn2_p[1][:, c], xn2[:, c], xn2_p[0][:, c].bitcast(F32), ALU.subtract).then_inc(xl_ok, 1)
            gate_copy(B - 1)
            gate_low(1)
            route_scores(1)
            route_weights(1)
            for v in range(2, len(UNITS)):
                gate_unit(v)
                gate_low(v)
            for h in range(NHALF):
                dve.wait_ge(y_ok, len(UNITS) - NHALF + h + 1)
                V.tensor_tensor(x1[:, h * HALF:(h + 1) * HALF], ps[:, YB + h, :], x1[:, h * HALF:(h + 1) * HALF],
                                ALU.add).then_inc(ot_ok, 1)

        @block.tensor
        def _(pe):
            T = nc.tensor
            READ = {"mean1": dif_ok[0], "mean2": dif_ok[1], "var1": var_ok[0], "var2": var_ok[1], "bc1": norm_ok[0],
                    "bc2": norm_ok[1], "shift": srow_ok, "wout": x1_ok, "gate": lg_ok, "oT": oT_ok, "cwT": cwT_ok}

            def misc_free(k):
                if k:
                    what, i = misc_all[k - 1]
                    pe.wait_ge(READ[what], i + 1)

            def misc_op(what, i):
                misc_free(misc_at[what, i])
                out = ps[:, MISC, :]
                if what in ("mean1", "mean2"):
                    src = xt if what == "mean1" else x1
                    if what == "mean1":
                        pe.wait_ge(*((x_in, 16) if i else (x0_in, 16)))
                    else:
                        pe.wait_ge(x1_ok, i + 1)
                    ins = T.matmul(out[:, 0:SQ], mean_w, src[:, SQ * i:SQ * (i + 1)], start=True, stop=True)
                if what in ("var1", "var2"):
                    z = int(what[-1]) - 1
                    pe.wait_ge(sq_ok[z], i + 1)
                    for t in range(QT):
                        ins = T.matmul(out[:, t:t + 1], sq[z][:, P * t:P * (t + 1)], mean_w[:, 0:1], start=True, stop=True)
                if what in ("bc1", "bc2"):
                    z = int(what[-1]) - 1
                    pe.wait_ge(diag_ok[z], i + 1)
                    ins = T.matmul(out[:, 0:SQ], ones, diag[z][:].rearrange("p t q -> p (t q)"), start=True, stop=True)
                if what == "shift":
                    pe.wait_ge(sp_ok, i + 1)
                    for t in range(QT):
                        ins = T.transpose(out[0:3 * GH, P // 2 * t:P // 2 * (t + 1)].bitcast(BF16),
                                          s_part[:, i % 2, t].rearrange("p r j -> p (r j)"), identb[:, 0, :])
                if what == "oT":
                    pe.wait_ge(on_ok, GROUPS * (i + 1))
                    for t in range(QT):
                        ins = T.transpose(out[:, P * t:P * (t + 1)], o_nat[:, t].rearrange("p h d -> p (h d)"), ident)
                if what == "wout":
                    if i == 0:
                        pe.wait_ge(wo_in, 32)
                    pe.wait_ge(oT_ok, i + 1)
                    ins = T.matmul(out[:, 0:SQ], wo_sb[:], oT[:], start=True, stop=True)
                if what == "gate":
                    if i == 0:
                        pe.wait_ge(gate_in, 32)
                    pe.wait_ge(norm_ok[1], i + 1)
                    for t in range(QT):
                        ins = T.matmul(out[:, E * t:E * (t + 1)], xn2[:, SQ * i + P * t:SQ * i + P * (t + 1)], gate_sb[:],
                                       start=True, stop=True)
                if what == "cwT":
                    pe.wait_ge(cw_ok, i + 1)
                    ins = T.transpose(out[0:E * HT, 0:P], cw[:].rearrange("p e t -> p (e t)"), ident)
                ins.then_inc(misc_written, 1)

            def max_scores(n, j):
                b, g = divmod(n, GROUPS)
                if g == 0 and j == 0:
                    pe.wait_ge(ones_ok[b % 2], 1)
                    pe.wait_ge(k_stacked[b % 2], 16 * SLOTS * (b // 2 + 1))
                    pe.wait_ge(q_stacked[b % 2], 16 * SLOTS * (b // 2 + 1))
                h = GH * g + j
                for t in range(QT):
                    r = QT * (GH * n + j) + t
                    if r >= QT:
                        pe.wait_ge(max_taken, r - QT + 1)
                    T.matmul(ps[:, MAXB + t, :], q_st[b % 2][:, h, P * t:P * (t + 1)], k_st[b % 2][:, h, :],
                             start=True, stop=True).then_inc(max_scored, 1)

            def scores(n, u):
                b, g = divmod(n, GROUPS)
                if u == 0:
                    pe.wait_ge(shift_in[n % 2], 16 * (n // 2 + 1))
                if KT * n + u >= 2:
                    pe.wait_ge(exp_ok, KT * n + u - 1)
                for a in range(2):
                    out = ps[:, 2 * (u % 2) + a, :]
                    for c in range(2):
                        h = GH * g + 2 * a + c
                        T.matmul(out[:, SQ * c:SQ * (c + 1)], k_st[b % 2][:, h, P * u:P * (u + 1)], q_st[b % 2][:, h, :],
                                 start=(c == 0), stop=False, skip_group_check=True)
                    for t in range(QT):
                        ins = T.matmul(out.rearrange("p (c q) -> p c q", c=2)[:, :, P * t:P * (t + 1)],
                                       mask_b[:, QT * b + t, P * u:P * (u + 1)], identb[:],
                                       start=False, stop=(t == QT - 1), skip_group_check=True)
                ins.then_inc(scored, 1)

            def values(n):
                pe.wait_ge(exp_ok, KT * (n + 1))
                pe.wait_ge(v_placed, n + 1)
                if n:
                    pe.wait_ge(on_ok, n)
                for u in range(KT):
                    for j in range(GH):
                        ins = T.matmul(ps[32 * j:32 * j + 32, PVB, 0:SQ], v_st[:, n % GROUPS, u, j, :],
                                       prob[n % 2][:, u, j, :], start=(u == 0), stop=(u == KT - 1),
                                       skip_group_check=True)
                ins.then_inc(pv_ok, 1)

            def transpose_out(n):
                pe.wait_ge(pv_copied, n + 1)
                for t in range(QT):
                    ins = T.transpose(ps[:, PVB, SQ + P * t:SQ + P * (t + 1)], pv_sb[:, P * t:P * (t + 1)], ident)
                ins.then_inc(pvt_ok, 1)

            pe.wait_ge(cst_in, 16)
            misc_op("mean1", 0)
            misc_op("var1", 0)
            misc_op("bc1", 0)
            pe.wait_ge(identb_ok, 2)
            for j in range(GH):
                max_scores(0, j)
            for j in range(GH):
                if j == 2:
                    misc_op("shift", 0)
                max_scores(1, j)
            pe.wait_ge(mask_ok, 1)
            for n in range(STEPS):
                for u in range(KT):
                    scores(n, u)
                    if u == 0 and n:
                        values(n - 1)
                    for op in misc_ops(n, u, "a"):
                        misc_op(*op)
                    if n + 2 < STEPS:
                        max_scores(n + 2, u)
                    if u == 1 and n:
                        transpose_out(n - 1)
                    for op in misc_ops(n, u, "b"):
                        misc_op(*op)

            def three(bank, lhs, rhs, start=True, stop=True):
                for k, (a, b) in enumerate([(0, 0), (0, 1), (1, 0)]):
                    ins = T.matmul(ps[:, bank, :], lhs[a], rhs[b], start=start and k == 0, stop=stop and k == 2,
                                   skip_group_check=True)
                return ins

            def w_part(v, first):
                w = w_p[UNITS[v][0] % W_SLOTS]
                return [w[r][:, first:first + P] for r in range(2)]

            def h1(v):
                e, h = UNITS[v]
                pe.wait_ge(wl_ok, e + 1)
                pe.wait_ge(xl_ok, 2 * (h + 1))
                pe.wait_ge(*((sil_ok, v) if v else (exp_ok, KT * STEPS - 1)))
                x = [xn2_p[r][:, HALF * h:HALF * (h + 1)] for r in range(2)]
                for m in range(MT):
                    ins = three(m, w_part(v, P * m), x)
                ins.then_inc(h1_ok, 1)

            def h3(v):
                h = UNITS[v][1]
                if v >= 2:
                    pe.wait_ge(gat_ok, v - 1)
                else:
                    pe.wait_ge(exp_ok, KT * STEPS)
                x = [xn2_p[r][:, HALF * h:HALF * (h + 1)] for r in range(2)]
                for m in range(MT):
                    ins = three(H3[v % 2] + m, w_part(v, INTER + P * m), x)
                ins.then_inc(h3_ok, 1)

            def down(v):
                e, h = UNITS[v]
                pe.wait_ge(gl_ok, v + 1)
                for m in range(MT):
                    ins = three(YB + h, w_part(v, 2 * INTER + P * m), [g_p[v % 2][r][:, m, :] for r in range(2)],
                                start=(e == 0 and m == 0), stop=(e == E and m == MT - 1))
                ins.then_inc(y_ok, 1)

            h1(0)
            values(STEPS - 1)
            transpose_out(STEPS - 1)
            h3(0)
            misc_op("oT", B - 1)
            h1(1)
            misc_op("wout", B - 1)
            h3(1)
            misc_op("mean2", B - 1)
            pe.wait_ge(on_ok, STEPS)
            down(0)
            misc_op("var2", B - 1)
            misc_op("bc2", B - 1)
            misc_op("gate", B - 1)
            down(1)
            for v in range(2, len(UNITS) + LAG):
                if v < len(UNITS):
                    h1(v)
                    h3(v)
                if v == 2:
                    misc_op("cwT", 1)
                    misc_free(len(misc_all))
                if v >= LAG + 2:
                    down(v - LAG)


def kernel(**inputs):
    import concourse.bacc as _bacc
    from concourse.bass_utils import run_bass_kernel_spmd as _run

    a = {k: np.asarray(v) for k, v in inputs.items()}
    order = np.arange(D).reshape(HEADS, DH).T.reshape(-1)

    def up(w, sw):
        return np.concatenate([sw[None], w]).transpose(0, 2, 1)[:, order]

    def down(w, sw):
        w = np.concatenate([sw[None], w])[:, order].transpose(0, 2, 1)
        return w.reshape(E + 1, MT, P, D).transpose(0, 2, 1, 3).reshape(E + 1, P, MT * D)

    ffn = np.concatenate([up(a["L0_ffn_w1"], a["L0_ffn_sw1"]), up(a["L0_ffn_w3"], a["L0_ffn_sw3"]),
                          down(a["L0_ffn_w2"], a["L0_ffn_sw2"])], axis=2)
    cst = np.zeros((P, C_W), np.float32)
    cst[:, C_ID:C_ID + P] = np.eye(P)
    cst[:, C_MEAN:C_MEAN + P] = 1.0 / D
    cst[:, C_ONE:C_ONE + P] = 1.0
    cst[:, C_LT:] = np.tril(np.ones((E, E)), -1).reshape(-1)
    arrays = {
        "xT": a["x"].reshape(TOK, D).T[order], "ctxT": a["ctx_1024"].transpose(0, 2, 1)[:, order],
        "ctx": a["ctx_1024"].reshape(B * SK, D), "mask": a["mask_Bx1xSxS2_ik1"].reshape(TOK, SK),
        "wo": a["L0_xattn_W_out"].T[:, order], "bo": a["L0_xattn_b_out"][order].reshape(D, 1),
        "gateT": a["L0_ffn_gate_w"].T[order], "gbias": a["L0_ffn_gate_bias"].reshape(1, E), "ffn": ffn, "cst": cst,
    }
    arrays = {f"in_{k}": np.ascontiguousarray(v) for k, v in arrays.items()}
    nc = _bacc.Bacc("TRN2", target_bir_lowering=False, num_devices=1)
    args = [nc.dram_tensor(k, v.shape, mybir.dt.from_np(v.dtype), kind="ExternalInput").ap() for k, v in arrays.items()]
    out = nc.dram_tensor("out_0_dram", (P, TOK), F32, kind="ExternalOutput").ap()
    comb = nc.dram_tensor("comb_dram", (E, TOK), F32, kind="Internal").ap()
    build(nc, *args, out, comb)
    r = _run(nc, [arrays], core_ids=[0])
    got = np.asarray(r.results[0]["out_0_dram"])
    y = np.empty((TOK, D), np.float32)
    y[:, order] = got.T
    return y.reshape(B, SQ, D)
```

```python
from contextlib import ExitStack

import numpy as np
import concourse.bass as bass
from concourse import mybir

F32 = mybir.dt.float32
BF16 = mybir.dt.bfloat16
I32 = mybir.dt.int32
U32 = mybir.dt.uint32
F32R = mybir.dt.float32r
ALU = mybir.AluOpType
ACT = mybir.ActivationFunctionType
AX = mybir.AxisListType

P = 128
B, SQ, D, SK = 4, 256, 128, 512
HEADS, DH = 16, 8
GH = 4
GROUPS = HEADS // GH
STEPS = B * GROUPS
KT = SK // P
QT = SQ // P
TOK = B * SQ
TT = TOK // P
E, INTER, TOPK = 8, 256, 2
MT = INTER // P
HALF = 512
NHALF = TOK // HALF
HT = HALF // P
EPS = 1e-5
MASKED = -99957650920014020608.0
SCALE = 1.0 / float(np.sqrt(DH))
LOWEST = -3.0e38
MINUS_ONES = 0xBF80BF80
K_PARTS = [0, 0, 0, 1, 1, 2]
Q_PARTS = [0, 1, 2, 0, 1, 0]
SLOTS = len(K_PARTS)
SHIFT_ROW = 64
SUM_ROW = DH
C_ID, C_LT = 0, P
C_W = P + E * E


W_SLOTS = 5
UNITS = ([(e, 0) for e in range(W_SLOTS)] + [(e, 1) for e in range(1, W_SLOTS)]
         + [(e, h) for e in range(W_SLOTS, E + 1) for h in range(NHALF)] + [(0, 1)])
LAST = len(UNITS) - 1
CUT = LAST - 1
LAG = 2


def routed(v):
    return sum(e > 0 for e, _ in UNITS[:v])


def split_behind(v):
    e = W_SLOTS + (v - W_SLOTS - LAG) // 2
    return e if v >= W_SLOTS + LAG and (v - W_SLOTS - LAG) % 2 == 0 and e <= E else None


def gated(v, m=MT - 1):
    return v + 1 if v < CUT else CUT + MT * (v - CUT) + m + 1


def slot(e):
    return 1 + (e - 1) % (W_SLOTS - 1) if e else 0


def last_unit(e):
    return max(v for v, (f, _) in enumerate(UNITS) if f == e)


def half_units(h):
    return [v for v, (_, g) in enumerate(UNITS) if g == h]


OUTPUTS = [(slice(0, HALF), half_units(0)[-1] + 1)] + [
    (slice(HALF + SQ * i, HALF + SQ * (i + 1)), LAST + 1) for i in range(HALF // SQ)]


def build(nc, xT, ctxT, ctx, mask, wo, bo, gateT, gbias, ffn, cst, outT, comb):
    with ExitStack() as st:
        def sb(name, shape, dt=F32):
            return st.enter_context(nc.sbuf_tensor(name, shape, dt))

        def sem(name):
            return st.enter_context(nc.semaphore(name))

        def sems(name, n=2):
            return [sem(f"{name}{i}") for i in range(n)]

        cs = sb("cs", [P, C_W])
        ident = cs[:, C_ID:C_ID + P]
        mean_w = sb("mean_w", [P, P])[:]
        ones = sb("ones", [P, P])[:]
        lower = cs[:, C_LT:C_LT + E * E]
        identb = sb("identb", [P, 2, P], BF16)
        xt = sb("xt", [P, TOK])
        kT = sb("kT", [P, B, SK])
        vN = sb("vN", [P, B * KT, D])
        mask_i = sb("mask_i", [P, 2 * QT, SK], I32)
        mask_b = sb("mask_b", [P, B * QT, SK], BF16)
        wo_sb = sb("wo_sb", [P, D])
        bo_sb = sb("bo_sb", [P, 1])
        gate_sb = sb("gate_sb", [P, E])
        gb_sb = sb("gb_sb", [P, E])
        k_part = sb("k_part", [P, 3, SK], BF16)
        q_part = sb("q_part", [P, 3, SQ], BF16)
        k_rest = sb("k_rest", [P, SK])
        q_rest = sb("q_rest", [P, SQ])
        k_st = [sb(f"k_st{i}", [P, HEADS, SK], BF16) for i in range(2)]
        q_st = [sb(f"q_st{i}", [P, HEADS, SQ], BF16) for i in range(2)]
        v_st = sb("v_st", [P, GROUPS, KT, GH, 32])
        junk = sb("junk", [P, QT, SK], BF16)
        rmax = sb("rmax", [P, 2, QT, GH])
        s_rest = sb("s_rest", [P, QT, GH])
        s_part = sb("s_part", [P, 2, QT, 3, GH], BF16)
        s_row = sb("s_row", [3 * GH, 2, SQ], BF16)
        prob = [sb(f"prob{i}", [P, KT, GH, SQ]) for i in range(2)]
        pv_sb = sb("pv_sb", [P, SQ])
        rsum = sb("rsum", [P, QT, GH])
        o_nat = sb("o_nat", [P, QT, HEADS, DH])
        oT = sb("oT", [P, SQ])
        dif = [sb(f"dif{i}", [P, SQ]) for i in range(2)]
        sq = [sb(f"sq{i}", [P, SQ]) for i in range(2)]
        vareps = [sb(f"vareps{i}", [P, QT]) for i in range(2)]
        rstd = [sb(f"rstd{i}", [P, QT]) for i in range(2)]
        diag = [sb(f"diag{i}", [P, QT, P]) for i in range(2)]
        mhalf = sb("mhalf", [P, QT])
        qn = sb("qn", [P, SQ])
        x1 = sb("x1", [P, TOK])
        xn2 = sb("xn2", [P, TOK])
        xn2_p = [sb(f"xn2_p{i}", [P, TOK], F32R) for i in range(2)]
        lg = sb("lg", [P, TT, E])
        r1 = sb("r1", [P, HT])
        ex = sb("ex", [P, HT, E])
        scr = sb("scr", [P, HT, E])
        bia = sb("bia", [P, HT, E])
        gtm = sb("gtm", [P, HT, E, E])
        eqm = sb("eqm", [P, HT, E, E])
        rank = sb("rank", [P, HT, E])
        cw = sb("cw", [P, E, HT])
        cwT = sb("cwT", [E * HT, P])
        w_raw = [sb(f"w_raw{i}", [P, 3 * INTER]) for i in range(2)]
        w_p = [[sb(f"w_p{i}_{r}", [P, 3 * INTER], F32R)[:] for r in range(2)] for i in range(W_SLOTS - 2)]
        words = k_st[0][:].rearrange("p h k -> p (h k)").bitcast(F32R)
        w_p += [[words[:, 3 * INTER * (2 * i + r):3 * INTER * (2 * i + r + 1)] for r in range(2)] for i in range(2)]
        g_p = [[sb(f"g_p{i}_{r}", [P, MT, HALF], F32R) for r in range(2)] for i in range(2)]

        def reuse(i):
            return prob[0][:, i].rearrange("p j q -> p (j q)")

        sil = [reuse(0), reuse(1)]
        gat = [reuse(2), reuse(3)]
        cb = [prob[1][:, i, 0:HALF // SQ].rearrange("p j q -> p (j q)") for i in range(3)]

        ps = st.enter_context(nc.psum_tensor("ps", [P, 8, 512], F32))
        MAXB, PVB, MISC = 4, 6, 7
        H3 = [2, 4]

        def max_bank(n, j, t):
            return (2 if n < 2 and j % 2 else MAXB) + t

        def H1(v):
            return 0 if v else MAXB
        YB = 6

        cst_in, x0_in, x_in, k0_in, k1_in, k_in, v_in, m0_in, m_in, wo_in, gate_in = [
            sem(n) for n in "cst_in x0_in x_in k0_in k1_in k_in v_in m0_in m_in wo_in gate_in".split()]
        k_stacked, q_stacked, shift_in = sems("k_stacked"), sems("q_stacked"), sems("shift_in")
        stack_zero, ones_ok = sems("stack_zero"), sems("ones_ok")
        consts_ok = sem("consts_ok")
        identb_ok, v_placed, v_zero, mask_ok = sem("identb_ok"), sem("v_placed"), sem("v_zero"), sem("mask_ok")
        kp_chain, kp_ok, qp_chain, qp_ok = sem("kp_chain"), sem("kp_ok"), sem("qp_chain"), sem("qp_ok")
        max_scored, max_taken = sem("max_scored"), sem("max_taken")
        sp_chain, sp_ok, srow_ok = sem("sp_chain"), sem("sp_ok"), sem("srow_ok")
        scored, exp_ok = sem("scored"), sem("exp_ok")
        pv_ok, pv_copied, pvt_ok, rsum_ok, on_ok = sem("pv_ok"), sem("pv_copied"), sem("pvt_ok"), sem("rsum_ok"), sem("on_ok")
        misc_written, oT_ok, x1_ok = sem("misc_written"), sem("oT_ok"), sem("x1_ok")
        dif_ok, sq_ok, var_ok = sems("dif_ok"), sems("sq_ok"), sems("var_ok")
        rstd_ok, diag_ok, norm_ok = sems("rstd_ok"), sems("diag_ok"), sems("norm_ok")
        xh_ok, xl_ok = sem("xh_ok"), sem("xl_ok")
        lg_ok, r_chain, ex_in, ex_ok, cw_ok, cwT_ok = (
            sem("lg_ok"), sem("r_chain"), sem("ex_in"), sem("ex_ok"), sem("cw_ok"), sem("cwT_ok"))
        comb_out = sem("comb_out")
        cb_in = sems("cb_in", 3)
        w_in = sems("w_in")
        wh_ok, wl_ok = sem("wh_ok"), sem("wl_ok")
        h1_ok, h3_ok, sil_ok, scaled_ok = sem("h1_ok"), sem("h3_ok"), sem("sil_ok"), sem("scaled_ok")
        gat_ok, gh_ok, gl0_ok, gl_ok, y_ok, ot_ok, out_done = (
            sem("gat_ok"), sem("gh_ok"), sem("gl0_ok"), sem("gl_ok"), sem("y_ok"), sem("ot_ok"), sem("out_done"))

        def low_ready(v, m=MT - 1):
            return (gl_ok, gated(v, m) - 1) if v else (gl0_ok, 1)

        def misc_ops(n, u, place):
            b, g = divmod(n, GROUPS)
            at = (g, u, place)
            ops = []
            if (u, place) == (1, "a") and n + 1 < STEPS:
                ops.append(("shift", n + 1))
            if (n, u, place) == (0, 0, "b"):
                ops.append(("bc1", 1))
            if b + 2 < B:
                ops += {(3, 0, "b"): [("mean1", b + 2)], (3, 2, "a"): [("var1", b + 2)],
                        (3, 3, "b"): [("bc1", b + 2)]}.get(at, [])
            if b:
                ops += {(1, 0, "a"): [("oT", b - 1)], (1, 0, "b"): [("wout", b - 1)], (1, 2, "a"): [("mean2", b - 1)],
                        (1, 3, "a"): [("var2", b - 1)], (2, 0, "b"): [("bc2", b - 1)],
                        (2, 2, "a"): [("gate", b - 1)]}.get(at, [])
            if (n, u, place) == CWT0:
                ops.append(("cwT", 0))
            return ops

        ROUTE0 = (GROUPS * 3 + 2, 0)
        CWT0 = (GROUPS * 3 + 3, 0, "b")
        VALUES_AT = {0: (0, 1), 1: (2, 3)}
        TURN_AT = 3
        SPLIT_AT = [(4, 1), (5, 0), (9, 0), (13, 0), (14, 1)]
        misc_all = [("mean1", 0), ("var1", 0), ("bc1", 0), ("mean1", 1), ("shift", 0), ("var1", 1)]
        for n in range(STEPS):
            for u in range(KT):
                misc_all += misc_ops(n, u, "a") + misc_ops(n, u, "b")
        misc_all += [(w, B - 1) for w in ("oT", "wout", "mean2", "var2", "bc2", "gate")] + [("cwT", 1)]
        misc_at = {op: i for i, op in enumerate(misc_all)}

        block = st.enter_context(nc.Block())

        @block.sync
        def _(sp):
            sp.dma_start(xt[:, 0:SQ], xT[:, 0:SQ]).then_inc(x0_in, 16)
            sp.dma_start(cs[:], cst).then_inc(cst_in, 16)
            sp.dma_start(mask_i[:, 0:QT, :], mask[0:SQ].rearrange("(t p) k -> p t k", p=P)).then_inc(m0_in, 16)

            sp.dma_start(kT[:, 1, :], ctxT[1]).then_inc(k1_in, 16)

            def stack(b):
                i = b % 2
                if b >= 2:
                    sp.wait_ge(scored, KT * GROUPS * (b - 1))
                else:
                    sp.wait_ge(stack_zero[i], 2)
                for parts, st, part_of, stacked, chain, done in (
                        (K_PARTS, k_st[i], k_part, k_stacked[i], kp_chain, kp_ok),
                        (Q_PARTS, q_st[i], q_part, q_stacked[i], qp_chain, qp_ok)):
                    for part, ready in enumerate([(chain, 3 * b + 1), (chain, 3 * b + 3), (done, b + 1)]):
                        sp.wait_ge(*ready)
                        for s in range(SLOTS):
                            if parts[s] == part:
                                sp.dma_start(st[DH * s:DH * s + DH, :, :], part_of[:, part, :]).then_inc(stacked, 16)

            stack(0)
            sp.dma_start(xt[:, SQ:], xT[:, SQ:]).then_inc(x_in, 16)
            sp.dma_start(mask_i[:, QT:, :], mask[SQ:2 * SQ].rearrange("(t p) k -> p t k", p=P)).then_inc(m_in, 16)
            for b in range(1, B):
                stack(b)
                if b == 1:
                    for e in range(2):
                        sp.dma_start(w_raw[e][:], ffn[e]).then_inc(w_in[e], 16)
                if b + 1 < B:
                    sp.wait_ge(mask_ok, b)
                    i = (b + 1) % 2
                    sp.dma_start(mask_i[:, QT * i:QT * (i + 1), :],
                                 mask[SQ * (b + 1):SQ * (b + 2)].rearrange("(t p) k -> p t k", p=P)
                                 ).then_inc((m0_in, m_in)[i], 16)

            def load_w(e):
                sp.wait_ge(wl_ok, e - 1)
                sp.dma_start(w_raw[e % 2][:], ffn[e]).then_inc(w_in[e % 2], 16)

            def load_cb(v):
                e, h = UNITS[v]
                k = routed(v)
                if k >= 3:
                    sp.wait_ge(scaled_ok, k - 2)
                sp.dma_start(cb[k % 3], comb[e - 1:e, HALF * h:HALF * (h + 1)].broadcast_to([P, HALF])
                             ).then_inc(cb_in[k % 3], 16)

            def store_comb(h):
                sp.wait_ge(cwT_ok, h + 1)
                sp.dma_start(comb[:, HALF * h:HALF * (h + 1)].rearrange("e (t p) -> e t p", p=P), cwT[:]
                             ).then_inc(comb_out, 16)
                sp.wait_ge(comb_out, 16 * (h + 1))

            for e in range(2, W_SLOTS):
                load_w(e)
            store_comb(0)
            load_w(W_SLOTS)
            sp.wait_ge(pv_ok, STEPS)
            for v in range(1, W_SLOTS):
                load_cb(v)
            store_comb(1)
            for v in range(W_SLOTS, LAST):
                load_cb(v)
                if split_behind(v) and split_behind(v) < E:
                    load_w(split_behind(v) + 1)
            for i, (c, _) in enumerate(OUTPUTS):
                sp.wait_ge(ot_ok, i + 1)
                sp.dma_start(outT[:, c], x1[:, c]).then_inc(out_done, 16)
            sp.wait_ge(out_done, 16 * len(OUTPUTS))

        @block.scalar
        def _(act):
            act.dma_start(kT[:, 0, :], ctxT[0]).then_inc(k0_in, 16)

            def square(i, b):
                act.wait_ge(dif_ok[i], b + 1)
                nc.scalar.activation(sq[i][:], dif[i][:], ACT.Square).then_inc(sq_ok[i], 1)

            square(0, 0)
            act.wait_ge(q_stacked[0], 16 * SLOTS)
            act.dma_start(vN[:], ctx.rearrange("(t p) d -> p t d", p=P)).then_inc(v_in, 16)

            def shift_row(n):
                b, g = divmod(n, GROUPS)
                act.wait_ge(misc_written, misc_at["shift", n] + 1)
                if n >= 2:
                    act.wait_ge(shift_in[n % 2], 16 * (n // 2))
                nc.scalar.copy(s_row[:, n % 2, :], ps[0:3 * GH, MISC, 0:SQ // 2].bitcast(BF16)).then_inc(srow_ok, 1)
                act.wait_ge(srow_ok, n + 1)
                if g == 0 and b >= 2:
                    act.wait_ge(scored, KT * GROUPS * (b - 1))
                if n == 0:
                    act.wait_ge(stack_zero[0], 2)
                if n == GROUPS:
                    act.wait_ge(stack_zero[1], 2)
                act.dma_start(q_st[b % 2][SHIFT_ROW:SHIFT_ROW + 3, GH * g:GH * g + GH, :], s_row[:, n % 2, :]
                              ).then_inc(shift_in[n % 2], 16)

            def pv_copy(n):
                act.wait_ge(pv_ok, n + 1)
                if n:
                    act.wait_ge(pvt_ok, n)
                nc.scalar.copy(pv_sb[:], ps[:, PVB, 0:SQ]).then_inc(pv_copied, 1)

            def oT_copy(b):
                act.wait_ge(misc_written, misc_at["oT", b] + 1)
                nc.scalar.copy(oT[:], ps[:, MISC, 0:SQ]).then_inc(oT_ok, 1)

            def cwT_copy(h):
                act.wait_ge(misc_written, misc_at["cwT", h] + 1)
                if h:
                    act.wait_ge(comb_out, 16 * h)
                nc.scalar.copy(cwT[:], ps[0:E * HT, MISC, 0:P]).then_inc(cwT_ok, 1)

            def route_exp(h):
                act.wait_ge(ex_in, h + 1)
                nc.scalar.activation(ex[:], ex[:], ACT.Exp).then_inc(ex_ok, 1)

            def x_high(b):
                act.wait_ge(norm_ok[1], b + 1)
                c = slice(SQ * b, SQ * (b + 1))
                nc.scalar.copy(xn2_p[0][:, c], xn2[:, c]).then_inc(xh_ok, 1)

            def w_high(e):
                act.wait_ge(w_in[e % 2], 16 * (e // 2 + 1))
                if e == 3:
                    act.wait_ge(scored, KT * GROUPS * (B - 1))
                if e >= W_SLOTS:
                    act.wait_ge(y_ok, last_unit(e - W_SLOTS + 1) + 1)
                nc.scalar.copy(w_p[slot(e)][0], w_raw[e % 2][:]).then_inc(wh_ok, 1)

            def misc_use(what, i):
                if what == "shift":
                    shift_row(i)
                if what == "mean1":
                    square(0, i)
                if what == "mean2":
                    square(1, i)
                if what == "oT":
                    oT_copy(i)
                if what == "cwT":
                    cwT_copy(i)

            square(0, 1)
            shift_row(0)
            act.dma_start(kT[:, 2:, :], ctxT[2:].rearrange("b d k -> d b k")).then_inc(k_in, 16)
            act.dma_start(wo_sb[:], wo).then_inc(wo_in, 16)
            act.dma_start(bo_sb[:], bo).then_inc(wo_in, 16)
            act.dma_start(gate_sb[:], gateT).then_inc(gate_in, 16)
            act.dma_start(gb_sb[:], gbias.broadcast_to([P, E])).then_inc(gate_in, 16)
            for n in range(STEPS):
                for u in range(KT):
                    act.wait_ge(scored, KT * n + u + 1)
                    if n >= 2 and u == 0:
                        act.wait_ge(pv_ok, n - 1)
                    bank = 2 * (u % 2)
                    nc.scalar.activation(prob[n % 2][:, u].rearrange("p j q -> p (j q)"),
                                         ps[:, bank:bank + 2, :].rearrange("p a q -> p (a q)"),
                                         ACT.Exp, scale=SCALE).then_inc(exp_ok, 1)
                    for op in misc_ops(n, u, "a"):
                        misc_use(*op)
                    if u == max(VALUES_AT) and n:
                        pv_copy(n - 1)
                    for op in misc_ops(n, u, "b"):
                        misc_use(*op)
                    if (n, u) == ROUTE0:
                        route_exp(0)
                    if (n, u) in SPLIT_AT:
                        w_high(SPLIT_AT.index((n, u)))

            def silu(v):
                act.wait_ge(h1_ok, v + 1)
                if v >= 2:
                    act.wait_ge(gat_ok, v - 1)
                nc.scalar.activation(sil[v % 2], ps[:, H1(v):H1(v) + MT, :].rearrange("p m t -> p (m t)"),
                                     ACT.Silu).then_inc(sil_ok, 1)

            def gate_high(v):
                act.wait_ge(gat_ok, v + 1)
                if v >= 2:
                    act.wait_ge(y_ok, v - 1)
                nc.scalar.copy(g_p[v % 2][0][:].rearrange("p m t -> p (m t)"), gat[v % 2]).then_inc(gh_ok, 1)

            pv_copy(STEPS - 1)
            silu(0)
            oT_copy(B - 1)
            silu(1)
            square(1, B - 1)
            gate_high(0)
            gate_high(1)
            silu(2)
            x_high(B - 1)
            route_exp(1)
            silu(3)
            gate_high(2)
            silu(4)
            gate_high(3)
            cwT_copy(1)
            for v in range(5, LAST):
                silu(v)
                gate_high(v - 1)
                if split_behind(v):
                    w_high(split_behind(v))

            def gate_high_tile(v, m):
                act.wait_ge(gat_ok, gated(v, m))
                if m == 0:
                    act.wait_ge(y_ok, v - 1)
                nc.scalar.copy(g_p[v % 2][0][:, m, :], gat[v % 2][:, HALF * m:HALF * (m + 1)]).then_inc(gh_ok, 1)

            for m in range(MT):
                gate_high_tile(CUT, m)
            for m in range(MT):
                act.wait_ge(h1_ok, LAST + m + 1)
                nc.scalar.activation(sil[LAST % 2][:, HALF * m:HALF * (m + 1)], ps[:, m, :], ACT.Silu).then_inc(sil_ok, 1)
            for m in range(MT):
                gate_high_tile(LAST, m)

        @block.gpsimd
        def _(pool):
            G = nc.gpsimd
            G.memset(mhalf[:], -0.5).then_inc(v_zero, 1)
            G.memset(k_st[0][:].bitcast(U32), 0).then_inc(stack_zero[0], 1)
            pool.wait_ge(stack_zero[0], 2)
            pool.wait_ge(v_zero, 1)

            def power(i, b):
                pool.wait_ge(var_ok[i], b + 1)
                G.tensor_tensor(rstd[i][:], vareps[i][:], mhalf[:], ALU.pow).then_inc(rstd_ok[i], 1)

            def split_q(b):
                pool.wait_ge(norm_ok[0], b + 1)
                pool.wait_ge(q_stacked[(b - 1) % 2], 16 * SLOTS * ((b - 1) // 2 + 1))
                G.tensor_copy(q_part[:, 0, :], qn[:]).then_inc(qp_chain, 1)
                pool.wait_ge(qp_chain, 3 * b + 1)
                G.tensor_tensor(q_rest[:], qn[:], q_part[:, 0, :], ALU.subtract).then_inc(qp_chain, 1)
                pool.wait_ge(qp_chain, 3 * b + 2)
                G.tensor_copy(q_part[:, 1, :], q_rest[:]).then_inc(qp_chain, 1)
                pool.wait_ge(qp_chain, 3 * b + 3)
                G.tensor_tensor(q_part[:, 2, :], q_rest[:], q_part[:, 1, :], ALU.subtract).then_inc(qp_ok, 1)

            def split_k(b):
                if b == 2:
                    pool.wait_ge(k_in, 16)
                pool.wait_ge(k_stacked[(b - 1) % 2], 16 * SLOTS * ((b - 1) // 2 + 1))
                G.tensor_copy(k_part[:, 0, :], kT[:, b, :]).then_inc(kp_chain, 1)
                pool.wait_ge(kp_chain, 3 * b + 1)
                G.tensor_tensor(k_rest[:], kT[:, b, :], k_part[:, 0, :], ALU.subtract).then_inc(kp_chain, 1)
                pool.wait_ge(kp_chain, 3 * b + 2)
                G.tensor_copy(k_part[:, 1, :], k_rest[:]).then_inc(kp_chain, 1)
                pool.wait_ge(kp_chain, 3 * b + 3)
                G.tensor_tensor(k_part[:, 2, :], k_rest[:], k_part[:, 1, :], ALU.subtract).then_inc(kp_ok, 1)

            def shift_parts(n):
                i = n % 2
                pool.wait_ge(max_taken, QT * GH * (n + 1))
                if n >= 2:
                    pool.wait_ge(srow_ok, n - 1)
                G.tensor_copy(s_part[:, i, :, 0, :], rmax[:, i]).then_inc(sp_chain, 1)
                pool.wait_ge(sp_chain, 3 * n + 1)
                G.tensor_tensor(s_rest[:], rmax[:, i], s_part[:, i, :, 0, :], ALU.subtract).then_inc(sp_chain, 1)
                pool.wait_ge(sp_chain, 3 * n + 2)
                G.tensor_copy(s_part[:, i, :, 1, :], s_rest[:]).then_inc(sp_chain, 1)
                pool.wait_ge(sp_chain, 3 * n + 3)
                G.tensor_tensor(s_part[:, i, :, 2, :], s_rest[:], s_part[:, i, :, 1, :],
                                ALU.subtract).then_inc(sp_ok, 1)

            def place_v(n):
                b, g = divmod(n, GROUPS)
                if n >= GROUPS:
                    pool.wait_ge(pv_ok, n - GROUPS + 1)
                G.tensor_copy(
                    v_st[:, g, :, :, 0:DH],
                    vN[:, KT * b:KT * b + KT, GH * DH * g:GH * DH * (g + 1)].rearrange("p t (j d) -> p t j d", d=DH)
                ).then_inc(v_placed, 1)

            def split_x(b):
                pool.wait_ge(norm_ok[1], b + 1)
                c = slice(SQ * b, SQ * (b + 1))
                G.tensor_copy(xn2_p[0][:, c], xn2[:, c]).then_inc(xh_ok, 1)
                pool.wait_ge(xh_ok, b + 1)
                G.tensor_tensor(xn2_p[1][:, c], xn2[:, c], xn2_p[0][:, c].bitcast(F32), ALU.subtract).then_inc(xl_ok, 1)

            def w_low(e):
                pool.wait_ge(wh_ok, e + 1)
                i = slot(e)
                G.tensor_tensor(w_p[i][1], w_raw[e % 2][:], w_p[i][0].bitcast(F32), ALU.subtract).then_inc(wl_ok, 1)

            power(0, 0)
            pool.wait_ge(rstd_ok[0], 1)
            G.memset(k_st[0][SHIFT_ROW:SHIFT_ROW + 3, :, :].bitcast(U32), MINUS_ONES).then_inc(ones_ok[0], 1)
            pool.wait_ge(ones_ok[0], 1)
            G.memset(v_st[:], 0.0).then_inc(v_zero, 1)
            pool.wait_ge(v_zero, 2)
            G.memset(v_st[:, :, :, :, SUM_ROW:SUM_ROW + 1], 1.0).then_inc(v_zero, 1)
            G.memset(k_st[1][:].bitcast(U32), 0).then_inc(stack_zero[1], 1)
            pool.wait_ge(stack_zero[1], 2)
            G.memset(k_st[1][SHIFT_ROW:SHIFT_ROW + 3, :, :].bitcast(U32), MINUS_ONES).then_inc(ones_ok[1], 1)
            pool.wait_ge(ones_ok[1], 1)
            pool.wait_ge(v_zero, 3)
            shift_parts(0)
            power(0, 1)
            shift_parts(1)
            pool.wait_ge(v_in, 16)
            place_v(0)
            split_q(1)
            for n in range(1, GROUPS):
                place_v(n)
            for n in range(STEPS):
                b, g = divmod(n, GROUPS)
                for u in range(KT):
                    for what, i in misc_ops(n, u, "a"):
                        if what == "var1":
                            power(0, i)
                        if what == "var2":
                            power(1, i)
                    if u == 3 and n + 2 < STEPS:
                        shift_parts(n + 2)
                    for what, i in misc_ops(n, u, "b"):
                        if what == "bc1" and i > 1:
                            split_q(i)
                        if what == "bc2":
                            split_x(i)
                    if u == 2 and n and n + GROUPS - 1 < STEPS:
                        place_v(n + GROUPS - 1)
                    if (g, u) == (2, 1) and b + 2 < B:
                        split_k(b + 2)
                    if (n, u) in SPLIT_AT:
                        w_low(SPLIT_AT.index((n, u)))

            def scale(v):
                k = routed(v)
                pool.wait_ge(cb_in[k % 3], 16 * (k // 3 + 1))
                pool.wait_ge(sil_ok, v + 1)
                s = sil[v % 2].rearrange("p (m t) -> p m t", m=MT)
                G.tensor_tensor(s, s, cb[k % 3].unsqueeze(1).broadcast_to([P, MT, HALF]), ALU.mult
                                ).then_inc(scaled_ok, 1)

            scale(1)
            power(1, B - 1)
            pool.wait_ge(gh_ok, 1)
            G.tensor_tensor(g_p[0][1][:].rearrange("p m t -> p (m t)"), gat[0],
                            g_p[0][0][:].bitcast(F32).rearrange("p m t -> p (m t)"), ALU.subtract).then_inc(gl0_ok, 1)
            scale(2)
            scale(3)
            scale(4)
            for v in range(5, LAST):
                scale(v)
                if split_behind(v):
                    w_low(split_behind(v))

        @block.vector
        def _(dve):
            V = nc.vector

            def norm_dif(i, b):
                src = (xt, x1)[i]
                dve.wait_ge(misc_written, misc_at[f"mean{i + 1}", b] + 1)
                if i == 1:
                    dve.wait_ge(x1_ok, b + 1)
                V.tensor_tensor(dif[i][:], src[:, SQ * b:SQ * (b + 1)], ps[:, MISC, 0:SQ],
                                ALU.subtract).then_inc(dif_ok[i], 1)

            def norm_var(i, b):
                dve.wait_ge(misc_written, misc_at[f"var{i + 1}", b] + 1)
                V.tensor_scalar(vareps[i][:], ps[:, MISC, 0:QT], EPS, None, ALU.add).then_inc(var_ok[i], 1)

            def norm_diag(i, b):
                dve.wait_ge(rstd_ok[i], b + 1)
                for t in range(QT):
                    ins = V.tensor_scalar(diag[i][:, t, :], ident, rstd[i][:, t:t + 1], None, ALU.mult)
                ins.then_inc(diag_ok[i], 1)

            def norm_out(i, b):
                dve.wait_ge(misc_written, misc_at[f"bc{i + 1}", b] + 1)
                if i == 0 and b:
                    dve.wait_ge(qp_ok, b)
                out = (qn[:], xn2[:, SQ * b:SQ * (b + 1)])[i]
                V.tensor_tensor(out, dif[i][:], ps[:, MISC, 0:SQ], ALU.mult).then_inc(norm_ok[i], 1)

            def masks(b):
                dve.wait_ge((m0_in, m_in)[b % 2], 16 * (b // 2 + 1))
                i = b % 2
                V.tensor_scalar(mask_b[:, QT * b:QT * (b + 1), :], mask_i[:, QT * i:QT * (i + 1), :], 0.0, MASKED,
                                ALU.is_equal, ALU.mult).then_inc(mask_ok, 1)

            def row_max(n, j, tiles=range(QT)):
                b = n // GROUPS
                if n >= 2 and j == 0 and tiles[0] == 0:
                    dve.wait_ge(sp_ok, n - 1)
                for t in tiles:
                    dve.wait_ge(max_scored, QT * (GH * n + j) + t + 1)
                    if (0, 0) < (n, j) <= (2, 0):
                        dve.wait_ge(max_taken, QT * (GH * n + j - 1) + t + 1)
                    V.tensor_tensor_reduce(out=junk[:, t, :], in0=ps[:, max_bank(n, j, t), :], in1=mask_b[:, QT * b + t, :],
                                           scale=1.0, scalar=LOWEST, op0=ALU.add, op1=ALU.max,
                                           accum_out=rmax[:, n % 2, t, j:j + 1]).then_inc(max_taken, 1)

            def normalize(n):
                b, g = divmod(n, GROUPS)
                dve.wait_ge(pvt_ok, n + 1)
                o = ps[:, PVB, SQ:2 * SQ].rearrange("p (t j d) -> p t j d", t=QT, j=GH)
                V.reciprocal(rsum[:], o[:, :, :, SUM_ROW]).then_inc(rsum_ok, 1)
                dve.wait_ge(rsum_ok, n + 1)
                if g == 0 and b:
                    dve.wait_ge(misc_written, misc_at["oT", b - 1] + 1)
                V.tensor_tensor(o_nat[:, :, GH * g:GH * (g + 1), :], o[:, :, :, 0:DH],
                                rsum[:].unsqueeze(3).broadcast_to([P, QT, GH, DH]), ALU.mult).then_inc(on_ok, 1)

            def residual(b):
                dve.wait_ge(misc_written, misc_at["wout", b] + 1)
                if b == 0:
                    dve.wait_ge(wo_in, 32)
                V.scalar_tensor_tensor(out=x1[:, SQ * b:SQ * (b + 1)], in0=ps[:, MISC, 0:SQ], scalar=bo_sb[:, 0:1],
                                       in1=xt[:, SQ * b:SQ * (b + 1)], op0=ALU.add, op1=ALU.add).then_inc(x1_ok, 1)

            def gate_copy(b):
                dve.wait_ge(misc_written, misc_at["gate", b] + 1)
                V.tensor_copy(lg[:, QT * b:QT * (b + 1), :],
                              ps[:, MISC, 0:QT * E].rearrange("p (t e) -> p t e", e=E)).then_inc(lg_ok, 1)

            def misc_use(what, i):
                if what in ("mean1", "mean2"):
                    norm_dif(int(what[-1]) - 1, i)
                if what in ("var1", "var2"):
                    norm_var(int(what[-1]) - 1, i)
                if what in ("bc1", "bc2"):
                    norm_out(int(what[-1]) - 1, i)
                if what == "wout":
                    residual(i)
                if what == "gate":
                    gate_copy(i)

            def split(part, rest, src, chain, done, before=0, high=True):
                if high:
                    V.tensor_copy(part[:, 0, :], src).then_inc(chain, 1)
                dve.wait_ge(chain, before + 1)
                V.tensor_tensor(rest[:], src, part[:, 0, :], ALU.subtract).then_inc(chain, 1)
                dve.wait_ge(chain, before + 2)
                V.tensor_copy(part[:, 1, :], rest[:]).then_inc(chain, 1)
                dve.wait_ge(chain, before + 3)
                V.tensor_tensor(part[:, 2, :], rest[:], part[:, 1, :], ALU.subtract).then_inc(done, 1)

            steps = [0]

            def link(ins):
                steps[0] += 1
                ins.then_inc(r_chain, 1)
                dve.wait_ge(r_chain, steps[0])

            def route_scores(h):
                dve.wait_ge(lg_ok, 2 * (h + 1))
                l = lg[:, HT * h:HT * (h + 1), :]
                link(V.tensor_reduce(r1[:], l, AX.X, ALU.max))
                V.tensor_tensor(ex[:], l, r1[:].unsqueeze(2).broadcast_to([P, HT, E]), ALU.subtract).then_inc(ex_in, 1)

            def route_weights(h):
                dve.wait_ge(ex_ok, h + 1)
                if h == 0:
                    dve.wait_ge(gate_in, 32)
                link(V.tensor_reduce(r1[:], ex[:], AX.X, ALU.add))
                link(V.reciprocal(r1[:], r1[:]))
                link(V.tensor_tensor(scr[:], ex[:], r1[:].unsqueeze(2).broadcast_to([P, HT, E]), ALU.mult))
                link(V.tensor_tensor(bia[:], scr[:], gb_sb[:].unsqueeze(1).broadcast_to([P, HT, E]), ALU.add))
                other = bia[:].unsqueeze(2).broadcast_to([P, HT, E, E])
                own = bia[:].unsqueeze(3).broadcast_to([P, HT, E, E])
                V.tensor_tensor(gtm[:], other, own, ALU.is_gt).then_inc(r_chain, 1)
                steps[0] += 1
                link(V.tensor_tensor(eqm[:], other, own, ALU.is_equal))
                link(V.tensor_tensor(eqm[:], eqm[:], lower.rearrange("p (a b) -> p a b", a=E).unsqueeze(1)
                                     .broadcast_to([P, HT, E, E]), ALU.mult))
                link(V.tensor_tensor(gtm[:], gtm[:], eqm[:], ALU.add))
                link(V.tensor_reduce(rank[:], gtm[:], AX.X, ALU.add))
                if h:
                    dve.wait_ge(misc_written, misc_at["cwT", h - 1] + 1)
                V.scalar_tensor_tensor(out=cw[:].rearrange("p e t -> p t e"), in0=rank[:], scalar=float(TOPK),
                                       in1=scr[:], op0=ALU.is_lt, op1=ALU.mult).then_inc(cw_ok, 1)

            V.memset(mean_w, 1.0 / D).then_inc(consts_ok, 1)
            V.memset(ones, 1.0).then_inc(consts_ok, 1)
            V.memset(q_st[0][:].bitcast(U32), 0).then_inc(stack_zero[0], 1)
            dve.wait_ge(x0_in, 16)
            norm_dif(0, 0)
            dve.wait_ge(k0_in, 16)
            V.tensor_copy(k_part[:, 0, :], kT[:, 0, :]).then_inc(kp_chain, 1)
            dve.wait_ge(kp_chain, 1)
            V.tensor_tensor(k_rest[:], kT[:, 0, :], k_part[:, 0, :], ALU.subtract).then_inc(kp_chain, 1)
            norm_var(0, 0)
            dve.wait_ge(kp_chain, 2)
            V.tensor_copy(k_part[:, 1, :], k_rest[:]).then_inc(kp_chain, 1)
            dve.wait_ge(kp_chain, 3)
            V.tensor_tensor(k_part[:, 2, :], k_rest[:], k_part[:, 1, :], ALU.subtract).then_inc(kp_ok, 1)
            dve.wait_ge(cst_in, 16)
            norm_diag(0, 0)
            V.tensor_copy(identb[:, 0, :], ident).then_inc(identb_ok, 1)
            V.tensor_copy(identb[:, 1, :], ident).then_inc(identb_ok, 1)
            dve.wait_ge(misc_written, misc_at["bc1", 0] + 1)
            V.tensor_tensor(q_part[:, 0, :], dif[0][:], ps[:, MISC, 0:SQ], ALU.mult).then_inc(qp_chain, 1)
            norm_out(0, 0)
            dve.wait_ge(norm_ok[0], 1)
            split(q_part, q_rest, qn[:], qp_chain, qp_ok, high=False)
            masks(0)
            V.memset(q_st[1][:].bitcast(U32), 0).then_inc(stack_zero[1], 1)
            dve.wait_ge(k1_in, 16)
            dve.wait_ge(k_stacked[0], 16 * SLOTS)
            split(k_part, k_rest, kT[:, 1, :], kp_chain, kp_ok, 3)
            dve.wait_ge(mask_ok, 1)
            for j in range(GH):
                row_max(0, j)
            misc_use("mean1", 1)
            row_max(1, 0)
            row_max(1, 1)
            row_max(1, 2)
            misc_use("var1", 1)
            row_max(1, 3)
            norm_diag(0, 1)
            for n in range(STEPS):
                b, g = divmod(n, GROUPS)
                for u in range(KT):
                    if n + 2 < STEPS:
                        if u == 0 and (n + 2) % GROUPS == 0:
                            dve.wait_ge(mask_ok, (n + 2) // GROUPS + 1)
                        row_max(n + 2, u, [0])
                    for op in misc_ops(n, u, "a"):
                        misc_use(*op)
                    if n + 2 < STEPS:
                        row_max(n + 2, u, [1])
                    if u == TURN_AT and n:
                        normalize(n - 1)
                    for op in misc_ops(n, u, "b"):
                        misc_use(*op)
                    if (g, u) == (0, 0) and b + 1 < B:
                        masks(b + 1)
                    if (g, u) == (3, 2) and b + 2 < B:
                        norm_diag(0, b + 2)
                    if (g, u) == (1, 3) and b:
                        norm_diag(1, b - 1)
                    if (n, u) == ROUTE0:
                        route_scores(0)
                    if (n, u) == (ROUTE0[0], ROUTE0[1] + 1):
                        route_weights(0)
            normalize(STEPS - 1)

            def gate_unit(v):
                dve.wait_ge(h3_ok, v + 1)
                if UNITS[v][0]:
                    dve.wait_ge(scaled_ok, routed(v + 1))
                else:
                    dve.wait_ge(sil_ok, v + 1)
                if v >= 2:
                    dve.wait_ge(*low_ready(v - 2))
                bank = H3[v % 2]
                V.tensor_tensor(gat[v % 2], sil[v % 2], ps[:, bank:bank + MT, :].rearrange("p m t -> p (m t)"),
                                ALU.mult).then_inc(gat_ok, 1)

            def gate_low(v):
                dve.wait_ge(gh_ok, v + 1)
                V.tensor_tensor(g_p[v % 2][1][:].rearrange("p m t -> p (m t)"), gat[v % 2],
                                g_p[v % 2][0][:].bitcast(F32).rearrange("p m t -> p (m t)"),
                                ALU.subtract).then_inc(gl_ok, 1)

            residual(B - 1)
            norm_dif(1, B - 1)
            gate_unit(0)
            norm_var(1, B - 1)
            gate_unit(1)
            norm_diag(1, B - 1)
            norm_out(1, B - 1)
            gate_low(1)
            c = slice(SQ * (B - 1), SQ * B)
            dve.wait_ge(xh_ok, B)
            V.tensor_tensor(xn2_p[1][:, c], xn2[:, c], xn2_p[0][:, c].bitcast(F32), ALU.subtract).then_inc(xl_ok, 1)
            gate_copy(B - 1)
            route_scores(1)
            gate_unit(2)
            route_weights(1)
            gate_low(2)
            gate_unit(3)
            gate_low(3)
            for v in range(4, CUT):
                gate_unit(v)
                gate_low(v)
            for v in range(CUT, LAST + 1):
                tiles = [slice(HALF * m, HALF * (m + 1)) for m in range(MT)]
                dve.wait_ge(h3_ok, v + 1)
                dve.wait_ge(*low_ready(v - 2))
                for m in range(MT):
                    if v == LAST:
                        dve.wait_ge(sil_ok, LAST + m + 1)
                    else:
                        dve.wait_ge(scaled_ok, routed(v + 1))
                    V.tensor_tensor(gat[v % 2][:, tiles[m]], sil[v % 2][:, tiles[m]], ps[:, H3[v % 2] + m, :],
                                    ALU.mult).then_inc(gat_ok, 1)
                for m in range(MT):
                    dve.wait_ge(gh_ok, gated(v, m))
                    V.tensor_tensor(g_p[v % 2][1][:, m, :], gat[v % 2][:, tiles[m]],
                                    g_p[v % 2][0][:, m, :].bitcast(F32), ALU.subtract).then_inc(gl_ok, 1)
            for c, y_there in OUTPUTS:
                dve.wait_ge(y_ok, y_there)
                h, first = divmod(c.start, HALF)
                V.tensor_tensor(x1[:, c], ps[:, YB + h, first:first + c.stop - c.start], x1[:, c], ALU.add).then_inc(ot_ok, 1)

        @block.tensor
        def _(pe):
            T = nc.tensor
            READ = {"mean1": dif_ok[0], "mean2": dif_ok[1], "var1": var_ok[0], "var2": var_ok[1], "bc1": norm_ok[0],
                    "bc2": norm_ok[1], "shift": srow_ok, "wout": x1_ok, "gate": lg_ok, "oT": oT_ok, "cwT": cwT_ok}

            def misc_free(k):
                if k:
                    what, i = misc_all[k - 1]
                    pe.wait_ge(READ[what], i + 1)

            def misc_op(what, i):
                misc_free(misc_at[what, i])
                out = ps[:, MISC, :]
                if what in ("mean1", "mean2"):
                    src = xt if what == "mean1" else x1
                    if what == "mean1":
                        pe.wait_ge(*((x_in, 16) if i else (x0_in, 16)))
                    else:
                        pe.wait_ge(x1_ok, i + 1)
                    ins = T.matmul(out[:, 0:SQ], mean_w, src[:, SQ * i:SQ * (i + 1)], start=True, stop=True)
                if what in ("var1", "var2"):
                    z = int(what[-1]) - 1
                    pe.wait_ge(sq_ok[z], i + 1)
                    for t in range(QT):
                        ins = T.matmul(out[:, t:t + 1], sq[z][:, P * t:P * (t + 1)], mean_w[:, 0:1], start=True, stop=True)
                if what in ("bc1", "bc2"):
                    z = int(what[-1]) - 1
                    pe.wait_ge(diag_ok[z], i + 1)
                    ins = T.matmul(out[:, 0:SQ], ones, diag[z][:].rearrange("p t q -> p (t q)"), start=True, stop=True)
                if what == "shift":
                    pe.wait_ge(sp_ok, i + 1)
                    for t in range(QT):
                        ins = T.transpose(out[0:3 * GH, P // 2 * t:P // 2 * (t + 1)].bitcast(BF16),
                                          s_part[:, i % 2, t].rearrange("p r j -> p (r j)"), identb[:, 0, :])
                if what == "oT":
                    pe.wait_ge(on_ok, GROUPS * (i + 1))
                    for t in range(QT):
                        ins = T.transpose(out[:, P * t:P * (t + 1)], o_nat[:, t].rearrange("p h d -> p (h d)"), ident)
                if what == "wout":
                    if i == 0:
                        pe.wait_ge(wo_in, 32)
                    pe.wait_ge(oT_ok, i + 1)
                    ins = T.matmul(out[:, 0:SQ], wo_sb[:], oT[:], start=True, stop=True)
                if what == "gate":
                    if i == 0:
                        pe.wait_ge(gate_in, 32)
                    pe.wait_ge(norm_ok[1], i + 1)
                    for t in range(QT):
                        ins = T.matmul(out[:, E * t:E * (t + 1)], xn2[:, SQ * i + P * t:SQ * i + P * (t + 1)], gate_sb[:],
                                       start=True, stop=True)
                if what == "cwT":
                    pe.wait_ge(cw_ok, i + 1)
                    ins = T.transpose(out[0:E * HT, 0:P], cw[:].rearrange("p e t -> p (e t)"), ident)
                ins.then_inc(misc_written, 1)

            def max_scores(n, j, tiles=range(QT)):
                b, g = divmod(n, GROUPS)
                if g == 0 and j == 0 and tiles[0] == 0:
                    pe.wait_ge(ones_ok[b % 2], 1)
                    pe.wait_ge(k_stacked[b % 2], 16 * SLOTS * (b // 2 + 1))
                    pe.wait_ge(q_stacked[b % 2], 16 * SLOTS * (b // 2 + 1))
                h = GH * g + j
                for t in tiles:
                    r = QT * (GH * n + j) + t
                    ring = QT * (2 if n < 2 or (n, j) == (2, 0) else 1)
                    if r >= ring:
                        pe.wait_ge(max_taken, r - ring + 1)
                    T.matmul(ps[:, max_bank(n, j, t), :], q_st[b % 2][:, h, P * t:P * (t + 1)], k_st[b % 2][:, h, :],
                             start=True, stop=True).then_inc(max_scored, 1)

            def scores(n, u):
                b, g = divmod(n, GROUPS)
                if u == 0:
                    pe.wait_ge(shift_in[n % 2], 16 * (n // 2 + 1))
                if (n, u) == (0, 1):
                    pe.wait_ge(max_taken, QT * GH * 2)
                if KT * n + u >= 2:
                    pe.wait_ge(exp_ok, KT * n + u - 1)
                for a in range(2):
                    out = ps[:, 2 * (u % 2) + a, :]
                    for c in range(2):
                        h = GH * g + 2 * a + c
                        T.matmul(out[:, SQ * c:SQ * (c + 1)], k_st[b % 2][:, h, P * u:P * (u + 1)], q_st[b % 2][:, h, :],
                                 start=(c == 0), stop=False, skip_group_check=True)
                    for t in range(QT):
                        ins = T.matmul(out.rearrange("p (c q) -> p c q", c=2)[:, :, P * t:P * (t + 1)],
                                       mask_b[:, QT * b + t, P * u:P * (u + 1)], identb[:],
                                       start=False, stop=(t == QT - 1), skip_group_check=True)
                ins.then_inc(scored, 1)

            def values(n, tiles):
                pe.wait_ge(exp_ok, KT * n + tiles[-1] + 1)
                if tiles[0] == 0:
                    pe.wait_ge(v_placed, n + 1)
                    if n:
                        pe.wait_ge(on_ok, n)
                for u in tiles:
                    for j in range(GH):
                        ins = T.matmul(ps[32 * j:32 * j + 32, PVB, 0:SQ], v_st[:, n % GROUPS, u, j, :],
                                       prob[n % 2][:, u, j, :], start=(u == 0), stop=(u == KT - 1),
                                       skip_group_check=True)
                if tiles[-1] == KT - 1:
                    ins.then_inc(pv_ok, 1)

            def transpose_out(n):
                pe.wait_ge(pv_copied, n + 1)
                for t in range(QT):
                    ins = T.transpose(ps[:, PVB, SQ + P * t:SQ + P * (t + 1)], pv_sb[:, P * t:P * (t + 1)], ident)
                ins.then_inc(pvt_ok, 1)

            def three(bank, lhs, rhs, start=True, stop=True):
                for k, (a, b) in enumerate([(0, 0), (0, 1), (1, 0)]):
                    ins = T.matmul(ps[:, bank, :], lhs[a], rhs[b], start=start and k == 0, stop=stop and k == 2,
                                   skip_group_check=True)
                return ins

            def w_part(v, first):
                w = w_p[slot(UNITS[v][0])]
                return [w[r][:, first:first + P] for r in range(2)]

            def h1(v, tiles=range(MT)):
                e, h = UNITS[v]
                pe.wait_ge(wl_ok, e + 1)
                pe.wait_ge(xl_ok, 2 * (h + 1))
                if v == 1:
                    pe.wait_ge(exp_ok, KT * STEPS - 1)
                if v > 1:
                    pe.wait_ge(sil_ok, v)
                x = [xn2_p[r][:, HALF * h:HALF * (h + 1)] for r in range(2)]
                for m in tiles:
                    ins = three(H1(v) + m, w_part(v, P * m), x)
                    if m == MT - 1 or v == LAST:
                        ins.then_inc(h1_ok, 1)

            pe.wait_ge(consts_ok, 2)
            misc_op("mean1", 0)
            misc_op("var1", 0)
            misc_op("bc1", 0)
            pe.wait_ge(identb_ok, 2)
            pe.wait_ge(cst_in, 16)
            for j in range(GH):
                max_scores(0, j)
            misc_op("mean1", 1)
            max_scores(1, 0)
            max_scores(1, 1)
            misc_op("shift", 0)
            max_scores(1, 2)
            misc_op("var1", 1)
            max_scores(1, 3)
            pe.wait_ge(mask_ok, 1)
            for n in range(STEPS):
                for u in range(KT):
                    if (n, u) == (STEPS - 1, 0):
                        pe.wait_ge(max_taken, QT * GH * STEPS)
                        h1(0)
                    if n + 2 < STEPS:
                        max_scores(n + 2, u, [0])
                    scores(n, u)
                    for op in misc_ops(n, u, "a"):
                        misc_op(*op)
                    if n + 2 < STEPS:
                        max_scores(n + 2, u, [1])
                    if u == TURN_AT and n:
                        transpose_out(n - 1)
                    if u in VALUES_AT and n:
                        values(n - 1, VALUES_AT[u])
                    for op in misc_ops(n, u, "b"):
                        misc_op(*op)

            def h3(v, tiles=range(MT)):
                h = UNITS[v][1]
                if v >= 2:
                    pe.wait_ge(gat_ok, v - 1)
                elif v == 1:
                    pe.wait_ge(sil_ok, 1)
                else:
                    pe.wait_ge(exp_ok, KT * STEPS)
                x = [xn2_p[r][:, HALF * h:HALF * (h + 1)] for r in range(2)]
                for m in tiles:
                    ins = three(H3[v % 2] + m, w_part(v, INTER + P * m), x)
                if tiles[-1] == MT - 1:
                    ins.then_inc(h3_ok, 1)

            def down(v):
                h = UNITS[v][1]
                for m in range(MT):
                    pe.wait_ge(*low_ready(v, m))
                    ins = three(YB + h, w_part(v, 2 * INTER + P * m), [g_p[v % 2][r][:, m, :] for r in range(2)],
                                start=(v == half_units(h)[0] and m == 0), stop=(v == half_units(h)[-1] and m == MT - 1))
                ins.then_inc(y_ok, 1)

            last = B - 1
            values(STEPS - 1, range(KT - 1))
            values(STEPS - 1, [KT - 1])
            h1(1, [0])
            transpose_out(STEPS - 1)
            h1(1, [1])
            misc_op("oT", last)
            h3(0, [0])
            misc_op("wout", last)
            h3(0, [1])
            misc_op("mean2", last)
            h3(1)
            misc_op("var2", last)
            h1(2)
            misc_op("bc2", last)
            h3(2)
            misc_op("gate", last)
            pe.wait_ge(on_ok, STEPS)
            down(0)
            h1(3)
            down(1)
            h3(3)
            h1(4)
            h3(4)
            down(2)
            misc_op("cwT", 1)
            misc_free(len(misc_all))
            h1(5)
            down(3)
            h3(5)
            for v in range(6, len(UNITS) + LAG):
                if v < LAST:
                    h1(v)
                    h3(v)
                if v == LAST:
                    h3(v)
                    h1(v)
                down(v - LAG)


def kernel(**inputs):
    import concourse.bacc as _bacc
    from concourse.bass_utils import run_bass_kernel_spmd as _run

    a = {k: np.asarray(v) for k, v in inputs.items()}
    order = np.arange(D).reshape(HEADS, DH).T.reshape(-1)

    def up(w, sw):
        return np.concatenate([sw[None], w]).transpose(0, 2, 1)[:, order]

    def down(w, sw):
        w = np.concatenate([sw[None], w])[:, order].transpose(0, 2, 1)
        return w.reshape(E + 1, MT, P, D).transpose(0, 2, 1, 3).reshape(E + 1, P, MT * D)

    ffn = np.concatenate([up(a["L0_ffn_w1"], a["L0_ffn_sw1"]), up(a["L0_ffn_w3"], a["L0_ffn_sw3"]),
                          down(a["L0_ffn_w2"], a["L0_ffn_sw2"])], axis=2)
    cst = np.zeros((P, C_W), np.float32)
    cst[:, C_ID:C_ID + P] = np.eye(P)
    cst[:, C_LT:] = np.tril(np.ones((E, E)), -1).reshape(-1)
    arrays = {
        "xT": a["x"].reshape(TOK, D).T[order], "ctxT": a["ctx_1024"].transpose(0, 2, 1)[:, order],
        "ctx": a["ctx_1024"].reshape(B * SK, D), "mask": a["mask_Bx1xSxS2_ik1"].reshape(TOK, SK),
        "wo": a["L0_xattn_W_out"].T[:, order], "bo": a["L0_xattn_b_out"][order].reshape(D, 1),
        "gateT": a["L0_ffn_gate_w"].T[order], "gbias": a["L0_ffn_gate_bias"].reshape(1, E), "ffn": ffn, "cst": cst,
    }
    arrays = {f"in_{k}": np.ascontiguousarray(v) for k, v in arrays.items()}
    nc = _bacc.Bacc("TRN2", target_bir_lowering=False, num_devices=1)
    args = [nc.dram_tensor(k, v.shape, mybir.dt.from_np(v.dtype), kind="ExternalInput").ap() for k, v in arrays.items()]
    out = nc.dram_tensor("out_0_dram", (P, TOK), F32, kind="ExternalOutput").ap()
    comb = nc.dram_tensor("comb_dram", (E, TOK), F32, kind="Internal").ap()
    build(nc, *args, out, comb)
    r = _run(nc, [arrays], core_ids=[0])
    got = np.asarray(r.results[0]["out_0_dram"])
    y = np.empty((TOK, D), np.float32)
    y[:, order] = got.T
    return y.reshape(B, SQ, D)
```
